# Optimizing a Trainium2 kernel written in Bass

```python
import numpy as np
import jax
import jax.numpy as jnp

def _softmax(x, axis=-1):
    return jax.nn.softmax(x, axis=axis)

def _gelu(x):
    return jax.nn.gelu(x, approximate=True)

def _silu(x):
    return jax.nn.silu(x)

def _sigmoid(x):
    return jax.nn.sigmoid(x)

def _layernorm(x, axis=-1, eps=1e-05):
    m = jnp.mean(x, axis=axis, keepdims=True)
    v = jnp.var(x, axis=axis, keepdims=True)
    return (x - m) / jnp.sqrt(v + eps)

def _scatter_add(tgt, idx, src, axis=0):
    return tgt.at[idx].add(src)

def _segment_sum(src, seg, n):
    return jax.ops.segment_sum(src, seg, n)
kernel_name = 'mk_gnn_ffn_d1_gnn_r32_bcf59e'

def setup_inputs(seed: int=0):
    np.random.seed(seed)
    _w = jnp.asarray

    def _rec_inputs():
        import jax
        import jax.numpy as jnp
        _gk = jax.random.key(seed)
        x = -0.0006008 + 1.001 * jax.random.normal(jax.random.fold_in(_gk, 1), (3125, 256), jnp.float32)
        src = jax.random.randint(jax.random.fold_in(_gk, 2), (50000,), 0, 3125, jnp.int32)
        dst = jax.random.randint(jax.random.fold_in(_gk, 3), (50000,), 0, 3125, jnp.int32)
        _o = jnp.argsort(dst, stable=True)
        src = src[_o]
        dst = dst[_o]
        edge_type_16 = jax.random.randint(jax.random.fold_in(_gk, 12), (50000,), 0, 16, jnp.int32)
        return (x, src, dst, edge_type_16)
    x, src, dst, edge_type_16 = _rec_inputs()

    def _L0_gnn_setup():
        import jax, jax.numpy as jnp
        import numpy as np
        from jax.ops import segment_sum
        N_NODES = 10000
        N_EDGES = 5000
        IN_FEAT = 256
        OUT_FEAT = 256
        NUM_RELS = 16

        def _inv_degree(idx, n):
            deg = segment_sum(jnp.ones(idx.shape[0], dtype=jnp.float32), idx, num_segments=n)
            return jnp.where(deg > 0, 1.0 / deg, 0.0)

        def _typed_pass(feat, W, bias, src_idx, dst_idx, etypes, norm_per_edge, n):
            proj = jnp.einsum('ni,rio->rno', feat, W)
            m = proj[etypes, src_idx] + bias
            m = m * norm_per_edge[:, None]
            return segment_sum(m, dst_idx, num_segments=n)
        key = jax.random.key(seed)
        ks = jax.random.split(key, 8)
        feat = jax.random.normal(ks[0], (N_NODES, IN_FEAT), dtype=jnp.float32)
        Wf = jax.random.normal(ks[1], (NUM_RELS, IN_FEAT, OUT_FEAT), dtype=jnp.float32)
        Wb = jax.random.normal(ks[2], (NUM_RELS, IN_FEAT, OUT_FEAT), dtype=jnp.float32)
        loop_weight = jax.random.normal(ks[3], (IN_FEAT, OUT_FEAT), dtype=jnp.float32)
        forward_bias = jnp.zeros((OUT_FEAT,), dtype=jnp.float32)
        backward_bias = jnp.zeros((OUT_FEAT,), dtype=jnp.float32)
        self_bias = jnp.zeros((OUT_FEAT,), dtype=jnp.float32)
        src = jax.random.randint(ks[4], (N_EDGES,), 0, N_NODES, dtype=jnp.int32)
        dst = jax.random.randint(ks[5], (N_EDGES,), 0, N_NODES, dtype=jnp.int32)
        etypes = jax.random.randint(ks[6], (N_EDGES,), 0, NUM_RELS, dtype=jnp.int32)
        return {'feat': feat, 'Wf': Wf, 'Wb': Wb, 'loop_weight': loop_weight, 'forward_bias': forward_bias, 'backward_bias': backward_bias, 'self_bias': self_bias, 'src': src, 'dst': dst, 'etypes': etypes, 'use_dis_weight': 0, 'drop_out': 0}
    _L0_gnn_all = _L0_gnn_setup()
    _L0_gnn_in = {k: v for k, v in _L0_gnn_all.items() if k in ('Wf', 'Wb', 'loop_weight', 'forward_bias', 'backward_bias', 'self_bias')}
    del _L0_gnn_all

    def _L0_ffn_setup():
        import jax, jax.numpy as jnp
        import numpy as np
        D_MODEL = 256
        N_EXPERTS = 16
        HIDDEN = 512
        SCALE = 0.02
        key = jax.random.key(seed)
        ks = jax.random.split(key, 5)
        x = jax.random.normal(ks[0], (4, 256, D_MODEL), dtype=jnp.float32)
        gate_w = jax.random.normal(ks[1], (D_MODEL, N_EXPERTS), dtype=jnp.float32) * SCALE
        gate_b = jnp.zeros((N_EXPERTS,), dtype=jnp.float32)
        w1 = jax.random.normal(ks[2], (N_EXPERTS, D_MODEL, HIDDEN), dtype=jnp.float32) * SCALE
        w2 = jax.random.normal(ks[3], (N_EXPERTS, D_MODEL, HIDDEN), dtype=jnp.float32) * SCALE
        w3 = jax.random.normal(ks[4], (N_EXPERTS, HIDDEN, D_MODEL), dtype=jnp.float32) * SCALE
        return {'x': x, 'gate_w': gate_w, 'gate_b': gate_b, 'w1': w1, 'w2': w2, 'w3': w3}
    _L0_ffn_all = _L0_ffn_setup()
    _L0_ffn_in = {k: v for k, v in _L0_ffn_all.items() if k in ('gate_w', 'gate_b', 'w1', 'w2', 'w3')}
    del _L0_ffn_all
    return {'x': x, 'src': src, 'dst': dst, 'edge_type_16': edge_type_16, 'L0_gnn_Wf': _L0_gnn_in['Wf'], 'L0_gnn_Wb': _L0_gnn_in['Wb'], 'L0_gnn_loop_weight': _L0_gnn_in['loop_weight'], 'L0_gnn_forward_bias': _L0_gnn_in['forward_bias'], 'L0_gnn_backward_bias': _L0_gnn_in['backward_bias'], 'L0_gnn_self_bias': _L0_gnn_in['self_bias'], 'L0_ffn_gate_w': _L0_ffn_in['gate_w'], 'L0_ffn_gate_b': _L0_ffn_in['gate_b'], 'L0_ffn_w1': _L0_ffn_in['w1'], 'L0_ffn_w2': _L0_ffn_in['w2'], 'L0_ffn_w3': _L0_ffn_in['w3']}

def reference(x, src, dst, edge_type_16, L0_gnn_Wf, L0_gnn_Wb, L0_gnn_loop_weight, L0_gnn_forward_bias, L0_gnn_backward_bias, L0_gnn_self_bias, L0_ffn_gate_w, L0_ffn_gate_b, L0_ffn_w1, L0_ffn_w2, L0_ffn_w3):
    import jax
    import jax.numpy as jnp

    def _L0_gnn_ref(feat, Wf, Wb, loop_weight, forward_bias, backward_bias, self_bias, src, dst, etypes, use_dis_weight, drop_out):
        import jax, jax.numpy as jnp
        import numpy as np
        from jax.ops import segment_sum
        N_NODES = 10000
        N_EDGES = 5000
        IN_FEAT = 256
        OUT_FEAT = 256
        NUM_RELS = 16

        def _inv_degree(idx, n):
            deg = segment_sum(jnp.ones(idx.shape[0], dtype=jnp.float32), idx, num_segments=n)
            return jnp.where(deg > 0, 1.0 / deg, 0.0)

        def _typed_pass(feat, W, bias, src_idx, dst_idx, etypes, norm_per_edge, n):
            proj = jnp.einsum('ni,rio->rno', feat, W)
            m = proj[etypes, src_idx] + bias
            m = m * norm_per_edge[:, None]
            return segment_sum(m, dst_idx, num_segments=n)
        n = feat.shape[0]
        norm_f = _inv_degree(dst, n)[dst]
        m_forward = _typed_pass(feat, Wf, forward_bias, src, dst, etypes, norm_f, n)
        norm_b = _inv_degree(src, n)[src]
        m_backward = _typed_pass(feat, Wb, backward_bias, dst, src, etypes, norm_b, n)
        s = feat @ loop_weight
        s = s + s + self_bias
        return s + m_forward + m_backward

    def _L0_ffn_ref(x, gate_w, gate_b, w1, w2, w3):
        import jax, jax.numpy as jnp
        import numpy as np
        D_MODEL = 256
        N_EXPERTS = 16
        HIDDEN = 512
        SCALE = 0.02
        n_experts = w1.shape[0]
        logits = jnp.einsum('bsd,de->bse', x, gate_w) + gate_b
        probs = jax.nn.softmax(logits, axis=-1)
        top_probs, top_idx = jax.lax.top_k(probs, 2)
        top_probs = top_probs / jnp.sum(top_probs, axis=-1, keepdims=True)
        dispatch = jnp.sum(jax.nn.one_hot(top_idx, n_experts, dtype=x.dtype) * top_probs[..., None], axis=-2)
        h1 = jnp.einsum('bsd,edh->bseh', x, w1)
        h2 = jnp.einsum('bsd,edh->bseh', x, w2)
        hidden = jax.nn.silu(h1) * h2
        expert_out = jnp.einsum('bseh,eho->bseo', hidden, w3)
        return jnp.einsum('bseo,bse->bso', expert_out, dispatch)
    x = x + _L0_gnn_ref(_layernorm(x, axis=-1), L0_gnn_Wf, L0_gnn_Wb, L0_gnn_loop_weight, L0_gnn_forward_bias, L0_gnn_backward_bias, L0_gnn_self_bias, src, dst, edge_type_16, 0, 0)
    x = x + _L0_ffn_ref(_layernorm(x, axis=-1)[None], L0_ffn_gate_w, L0_ffn_gate_b, L0_ffn_w1, L0_ffn_w2, L0_ffn_w3)[0]
    return x

_drawn_inputs = setup_inputs


def setup_inputs(seed=0):
    import zlib

    import numpy as np

    out = dict(_drawn_inputs(seed))
    spreads = {'L0_gnn_forward_bias': (0.0, 0.8),
     'L0_gnn_backward_bias': (0.0, 0.8),
     'L0_gnn_self_bias': (0.0, 0.8),
     'L0_ffn_gate_b': (0.0, 0.8)}
    factors = {'L0_ffn_gate_w': 8.0, 'L0_ffn_w1': 8.0, 'L0_ffn_w2': 8.0, 'L0_ffn_w3': 8.0}
    for name, (base, spread) in spreads.items():
        noise = np.random.default_rng([zlib.crc32(name.encode()), seed]).standard_normal(out[name].shape)
        drawn = base * np.exp(spread * noise) if base else spread * noise
        out[name] = jnp.asarray(drawn.astype(out[name].dtype))
    for name, factor in factors.items():
        out[name] = (out[name] * factor).astype(out[name].dtype)
    return out
```

```python
import concourse.bass as bass
from concourse import mybir
from contextlib import ExitStack

fp32 = mybir.dt.float32
f16 = mybir.dt.float16
i32 = mybir.dt.int32
i16 = mybir.dt.int16
u16 = mybir.dt.uint16
ALU = mybir.AluOpType
ACT = mybir.ActivationFunctionType
AX = mybir.AxisListType
ds = bass.ds

P = 128
N = 3125
D = 256
KD = D // P
NT = (N + P - 1) // P
LAST = N - (NT - 1) * P
R = 16
E = 50000
EP, EC = 125, 400
assert EP * EC == E
CH = 416
assert CH >= (E + NT * (P - 1)) // P and CH % 16 == 0
AW = D + 2
HALF = R // 2
WH = HALF * KD * D
ST = 4
MR = 8
SR = 8
OR = 4
LEAD = 4
PRE = 15
A_SORT = EC // (NT - PRE)
B_SORT = EC // NT
NE = 16
H = 512
KH = H // P
NST = (2 * N + NE * (P - 1)) // P
NA = 2 * NT
EPS = 1e-5
SRC_BIAS = 1562.0
EXP_MASK = 0x7F800000
EXP_TWICE_BIAS = float(0x7F000000)


class Chain:

    def __init__(self, eng, sem):
        self.eng, self.sem, self.n = eng, sem, 0

    def mark(self, ins):
        ins.then_inc(self.sem, 1)
        self.n = self.n + 1

    def link(self, ins):
        self.mark(ins)
        self.eng.wait_ge(self.sem, self.n)


def build(nc, x, src, dst, typ, Wf, Wb, loopw, fbias, bbias, sbias, gate_w, gate_b, w1, w2, w3, out):
    ctx = ExitStack()
    with ctx:
        def sb(name, shape, dt=fp32):
            return ctx.enter_context(nc.sbuf_tensor(name, shape, dt))

        def sem(name):
            return ctx.enter_context(nc.semaphore(name))

        table = [nc.dram_tensor(f"messages_{n}", (NT * P * R, D), fp32).ap() for n in ("fwd", "bwd")]
        xs_dram = nc.dram_tensor("slot_rows", (NST * P, D), fp32).ap()
        ys_dram = nc.dram_tensor("slot_results", (NST * P, D), fp32).ap()

        x_sb = sb("x_sb", [P, NT, D])
        acc = [sb("acc_f", [P, NT * AW]), sb("acc_b", [P, NT * AW])]
        f_hi = sb("f_hi", [P, KD, NT * P], f16)
        f_lo = sb("f_lo", [P, KD, NT * P], f16)
        w_hi = sb("w_hi", [P, 2, 2 * WH], f16)
        w_lo = sb("w_lo", [P, 2, 2 * WH], f16)
        stage = sb("stage", [P, 2, ST * D])
        msg = sb("msg", [P, MR, AW])
        onehot = sb("onehot", [P, SR, P])
        ops_b = sb("ops_b", [EP, OR, CH], f16)
        ops_a = sb("ops_a", [EP, OR, 2, P], f16)
        slot_row = [sb(f"slot_row_{n}", [P, CH], i32) for n in "fb"]
        slot_loc = [sb(f"slot_loc_{n}", [P, CH], f16) for n in "fb"]
        tile_at = [sb(f"tile_at_{n}", [1, CH], i16) for n in "fb"]
        idx_now = sb("idx_now", [P, 2, 8], i32)
        iota_ch = sb("iota_ch", [P, CH], f16)
        iota_p = sb("iota_p", [P, P])
        iota_p16 = sb("iota_p16", [P, P], f16)
        iota_row = sb("iota_row", [P, 1])
        ident = sb("ident", [P, P])
        before = sb("before", [P, P])
        upto = sb("upto", [P, P])
        ones = sb("ones", [P, P])
        zeros16 = sb("zeros16", [1, P], f16)
        loop_hi = sb("loop_hi", [P, KD * D], f16)
        loop_lo = sb("loop_lo", [P, KD * D], f16)
        bias_f = sb("bias_f", [P, D])
        bias_b = sb("bias_b", [P, D])
        gw = sb("gw", [P, KD, NE])
        gb = sb("gb", [P, NE])
        eps = sb("eps", [P, 1])
        wscale = sb("wscale", [P, 5, 4])
        stats = sb("stats", [P, NT, 6])
        st = sb("st", [P, 6, NT])
        mean, rstd = st[:, 0], st[:, 1]
        small = sb("small", [P, 12, 32])
        small_i = sb("small_i", [P, 2, 32], i32)

        w_raw = acc[0][:, 0:WH]
        loop_raw = acc[0][:, WH:WH + KD * D]
        xn = acc[0][:, WH + KD * D:WH + KD * D + 5 * D].rearrange("p (j d) -> p j d", j=5)

        bias_s = acc[0][:, WH + (KD + 5) * D:WH + (KD + 6) * D]

        def edge(k):
            return acc[1][0:EP, k * EC:(k + 1) * EC]
        pos_b, pos_a = [edge(0), edge(4)], [edge(1), edge(5)]
        pay_1, pay_2 = [edge(2), edge(6)], [edge(3), edge(7)]
        e_src, e_dst, e_typ = edge(8).bitcast(i32), edge(9).bitcast(i32), edge(10).bitcast(i32)
        e_int, e_scan, e_pos = edge(11).bitcast(i32), edge(12), edge(13)
        e_key = edge(14).bitcast(f16)[:, 0:EC]
        e_eq = edge(15).bitcast(f16).rearrange("p (a b) -> p a b", a=2)
        assert 16 * EC <= NT * AW
        wbase = w_hi[:, :, :].rearrange("p a b -> p (a b)").bitcast(fp32)
        wbase2 = w_lo[:, :, :].rearrange("p a b -> p (a b)").bitcast(fp32)
        ew1 = [wbase[:, n * KD * H:(n + 1) * KD * H].rearrange("p (k h) -> p k h", k=KD) for n in range(2)]
        ew2 = [wbase[:, (2 + n) * KD * H:(3 + n) * KD * H].rearrange("p (k h) -> p k h", k=KD) for n in range(2)]
        ew3 = [wbase[:, (4 + n) * KD * H:(5 + n) * KD * H].rearrange("p (c d) -> p c d", c=KH) for n in range(2)]
        xs_in = [wbase2[:, n * D:(n + 1) * D] for n in range(2)]
        xs_t = [wbase2[:, (2 + n) * D:(3 + n) * D].rearrange("p (k s) -> p k s", k=KD) for n in range(2)]
        h_act = [wbase2[:, (4 + 2 * n) * D:(6 + 2 * n) * D] for n in range(2)]
        h_out = [wbase2[:, (8 + 2 * n) * D:(10 + 2 * n) * D].rearrange("p (c s) -> p c s", c=KH) for n in range(2)]
        y_sb = [wbase2[:, (12 + n) * D:(13 + n) * D] for n in range(2)]
        g0 = 14 * D
        gate = [wbase2[:, g0 + n * NT * NE:g0 + (n + 1) * NT * NE].rearrange("p (t e) -> p t e", e=NE) for n in range(6)]
        assert g0 + 6 * NT * NE <= 2 * WH
        xn2 = acc[0][:, 0:NT * D].rearrange("p (t d) -> p t d", d=D)
        xn2_t = f_hi[:, :, :].rearrange("p k n -> p (k n)").bitcast(fp32)[:, 0:4 * KD * P].rearrange(
            "p (j k s) -> p j k s", j=4, k=KD)
        fl = f_lo[:, :, :].rearrange("p k n -> p (k n)").bitcast(fp32)
        assign = fl[:, 0:NE * NA].rearrange("p (e j) -> p e j", e=NE)
        a_scan = fl[:, NE * NA:2 * NE * NA].rearrange("p (e j) -> p e j", e=NE)
        a_pos = fl[:, 2 * NE * NA:2 * NE * NA + NA]
        a_slot = fl[:, 2 * NE * NA + NA:2 * NE * NA + 2 * NA].bitcast(i32)
        prob = [fl[:, 2 * NE * NA + (2 + n) * NA:2 * NE * NA + (2 + n) * NA + NT] for n in range(8)]
        valid = sb("valid", [P, NT])
        fence_cell = sb("fence_cell", [1, 1])
        expert_at = sb("expert_at", [1, NST], i32)
        y_in = acc[1][:, 0:8 * D].rearrange("p (j d) -> p j d", j=8)

        onehot_flat = onehot[:, :, :].rearrange("p a b -> p (a b)")

        ps = ctx.enter_context(nc.psum_tensor("ps", [P, 8, 512], fp32))
        sort_ps = [ps[:, 4, 0:CH], ps[:, 5, 0:CH]]
        seg_ps = [ps[:, 6, 0:AW], ps[:, 7, 0:AW]]
        rank_ps = ps[:, 6, :]

        s_x = sem("x_loaded")
        s_xl = sem("x_tail_loaded")
        s_w = [sem(f"weights_loaded_{n}") for n in range(4)]
        s_lw = sem("loop_weights_loaded")
        s_edges = sem("edges_loaded")
        s_rows = sem("bias_rows_loaded")
        s_zero_st = sem("slot_rows_zeroed")
        s_const = sem("constants_ready")
        s_clear = sem("accumulator_cleared")
        s_dve = sem("dve_steps")
        s_pool = sem("pool_steps")
        s_act = sem("act_steps")
        s_pe = sem("pe_steps")
        s_wmax = sem("weight_max_ready")
        s_wall = sem("weight_max_reduced")
        s_wsc = sem("weight_scale_ready")
        s_whi = sem("weights_hi_ready")
        s_wlo = sem("weights_lo_ready")
        s_var = sem("variance_ready")
        s_std = sem("std_ready")
        s_xn = sem("xn_ready")
        s_xt = sem("xn_transposed")
        s_fhi = sem("f_hi_ready")
        s_flo = sem("f_lo_ready")
        s_loop = sem("loop_product_ready")
        s_base = sem("loop_product_used")
        s_cnt = sem("counts_ready")
        s_tot = sem("totals_ready")
        s_inc = sem("group_ends_ready")
        s_incp = sem("group_end_sums_ready")
        s_cmp = sem("chunk_compare_ready")
        s_map = sem("chunk_map_ready")
        s_proj = sem("projection_ready")
        s_evac = sem("projection_staged")
        s_free = sem("stage_free")
        s_out = [sem(f"stage_stored_{n}") for n in range(2)]
        s_ops = sem("sort_operands_ready")
        s_used = sem("sort_operands_used")
        s_sorted = sem("sort_finished")
        s_slots = sem("slot_tables_ready")
        s_ones = sem("message_ones_ready")
        s_gath = [sem(f"gathered_{n}") for n in range(MR)]
        s_turn = sem("gather_turns")
        s_hot = sem("onehot_ready")
        s_seg = sem("chunk_summed")
        s_acc = sem("chunk_added")
        s_x1 = sem("x1_ready")
        s_x2t = sem("xn2_transposed")
        s_x2c = sem("xn2_t_copied")
        s_gate = sem("logits_ready")
        s_exp = sem("exp_ready")
        s_sub = sem("exp_input_ready")
        s_slot2 = sem("token_slots_ready")
        s_scat = [sem(f"rows_scattered_{n}") for n in range(4)]
        s_allscat = sem("all_rows_scattered")
        s_ew = [sem(f"expert_weights_loaded_{n}") for n in range(2)]
        s_xsin = [sem(f"slot_rows_loaded_{n}") for n in range(2)]
        s_mt = sem("slot_tile_transposed")
        s_mtc = sem("slot_tile_t_copied")
        s_h = sem("hidden_ready")
        s_silu = sem("silu_ready")
        s_hm = sem("hidden_gated")
        s_y = sem("expert_result_ready")
        s_yc = sem("expert_result_copied")
        s_yo = [sem(f"expert_result_stored_{n}") for n in range(2)]
        s_yf = sem("expert_result_buffer_free")
        s_yg = [sem(f"results_gathered_{n}") for n in range(4)]
        s_fin = sem("output_rows_ready")
        s_st = sem("outputs_stored")

        block = ctx.enter_context(nc.Block())

        raw_types = w_raw.rearrange("p (t c) -> p t c", t=HALF)

        def half(W, h):
            return W[h * HALF:(h + 1) * HALF].rearrange("t (p k) o -> p t (k o)", k=KD)

        @block.sync
        def _(sp):
            sp.dma_start(raw_types, half(Wf, 0)).then_inc(s_w[0], 16)
            sp.wait_ge(s_wlo, 2)
            sp.dma_start(raw_types, half(Wf, 1)).then_inc(s_w[1], 16)
            for d in range(2):
                rows = table[d].rearrange("(n r) d -> n (r d)", r=R)
                if d == 0:
                    sp.sem_inc(s_free, 2)
                with sp.Fori(0, NT) as i:
                    for h in range(4):
                        sp.wait_ge(s_evac, i * 8 + (4 + d * NT * 8 + 2 * h + 2))
                        sp.dma_start(rows[ds(i * P, P), h * ST * D:(h + 1) * ST * D],
                                     stage[:, h % 2, :]).then_inc(s_out[h % 2], 16)
                        sp.wait_ge(s_out[h % 2], i * 32 + (d * NT * 32 + 16 * (h // 2) + 16))
                        sp.sem_inc(s_free, 1)
            sp.wait_ge(s_allscat, 1)
            sp.wait_ge(s_map, 3)
            with sp.Fori(0, NST // 2) as i:
                for n in range(2):
                    e = sp.value_load(expert_at[0:1, ds(i * 2 + n, 1)], min_val=0, max_val=NE - 1)
                    sp.wait_ge(s_y, i * 2 + (n + 1))
                    sp.dma_start(ew1[n], w1[ds(e, 1)].rearrange("e (p k) h -> (e p) k h", k=KD)).then_inc(s_ew[n], 16)
                    sp.dma_start(ew2[n], w2[ds(e, 1)].rearrange("e (p k) h -> (e p) k h", k=KD)).then_inc(s_ew[n], 16)
                    sp.dma_start(ew3[n], w3[ds(e, 1)].rearrange("e (p c) d -> (e p) c d", c=KH)).then_inc(s_ew[n], 16)
                    sp.dma_start(xs_in[n], xs_dram[ds((i * 2 + n) * P, P), :]).then_inc(s_xsin[n], 16)
            for t in range(NT):
                rows = P if t < NT - 1 else LAST
                sp.wait_ge(s_fin, t + 1)
                sp.dma_start(out[t * P:t * P + rows, :], x_sb[0:rows, t, :]).then_inc(s_st, 16)
            sp.wait_ge(s_st, 16 * NT)

        @block.scalar
        def _(act):
            act.dma_start(x_sb[:, 0:NT - 1, :], x[0:(NT - 1) * P].rearrange("(t p) d -> p t d", p=P)).then_inc(s_x, 16)
            act.wait_ge(s_const, 6)
            act.dma_start(x_sb[0:LAST, NT - 1, :], x[(NT - 1) * P:N]).then_inc(s_xl, 16)
            act.dma_start(loop_raw.rearrange("p (k o) -> p k o", k=KD), loopw.rearrange("(p k) o -> p k o", k=KD)).then_inc(s_lw, 16)
            for a, b in ((e_src, src), (e_dst, dst), (e_typ, typ)):
                act.dma_start(a, b.rearrange("(p c) -> p c", c=EC)).then_inc(s_edges, 16)
            for a, b in ((bias_f[:], fbias), (bias_b[:], bbias), (bias_s, sbias)):
                act.dma_start(a, b.partition_broadcast(P)).then_inc(s_rows, 16)
            act.dma_start(gb[:], gate_b.partition_broadcast(P)).then_inc(s_rows, 16)
            act.dma_start(gw[:], gate_w.rearrange("(p k) e -> p k e", k=KD)).then_inc(s_rows, 16)
            act.wait_ge(s_var, 1)
            nc.scalar.activation(st[:, 1], st[:, 2], ACT.Sqrt, bias=eps[:, 0:1]).then_inc(s_std, 1)
            act.wait_ge(s_wsc, 1)
            nc.scalar.activation(loop_hi[:], loop_raw, ACT.Copy, scale=wscale[:, 4, 3:4]).then_inc(s_whi, 1)
            with act.Fori(0, 5) as i:
                for j in range(5):
                    act.wait_ge(s_xt, i * 5 + (j + 1))
                    nc.scalar.copy(f_hi[:, :, ds((i * 5 + j) * P, P)],
                                   ps[:, j, 0:D].rearrange("p (k n) -> p k n", k=KD)).then_inc(s_fhi, 1)
            for n in range(2):
                act.wait_ge(s_wsc, n + 2)
                nc.scalar.activation(w_hi[:, 0, n * WH:(n + 1) * WH], w_raw, ACT.Copy,
                                     scale=wscale[:, n, 3:4]).then_inc(s_whi, 1)
            act.sem_inc(s_evac, 4)
            for d in range(2):
                with act.Fori(0, NT) as i:
                    for b in range(8):
                        if b % 2 == 0:
                            act.wait_ge(s_free, i * 4 + (d * NT * 4 + b // 2 + 1))
                        act.wait_ge(s_proj, i * 8 + (d * NT * 8 + b + 1))
                        nc.scalar.activation(stage[:, (b // 2) % 2, (b % 2) * 512:(b % 2 + 1) * 512], ps[:, b % 4, :],
                                             ACT.Copy, scale=wscale[:, 2 * d + b // 4, 2:3]).then_inc(s_evac, 1)
            act.wait_ge(s_var, 2)
            nc.scalar.activation(st[:, 1], st[:, 2], ACT.Sqrt, bias=eps[:, 0:1]).then_inc(s_std, 1)
            act.sem_inc(s_x2c, 4)
            for t in range(NT):
                act.wait_ge(s_x2t, t + 1)
                nc.scalar.copy(xn2_t[:, t % 4], ps[:, t % 4, 0:D].rearrange("p (k n) -> p k n", k=KD)).then_inc(s_x2c, 1)
            act.wait_ge(s_sub, 1)
            nc.scalar.activation(gate[2], gate[1], ACT.Exp).then_inc(s_exp, 1)
            with act.Fori(0, NST // 2) as i:
                for n in range(2):
                    act.wait_ge(s_h, i * 2 + (n + 1))
                    act.wait_ge(s_hm, i * 2 + (n + 1))
                    nc.scalar.activation(h_act[n], ps[:, 2 + 2 * n, :], ACT.Silu).then_inc(s_silu, 1)
                    act.wait_ge(s_yf, i * 2 + (n + 1))
                    act.wait_ge(s_y, i * 2 + (n + 3))
                    nc.scalar.copy(y_sb[n], ps[:, 6 + n, 0:D]).then_inc(s_yc, 1)

        @block.gpsimd
        def _(pool):
            chain = Chain(pool, s_pool)
            nc.gpsimd.iota(iota_p[:], [[1, P]], base=0, channel_multiplier=0,
                           allow_small_or_imprecise_dtypes=True).then_inc(s_const, 1)
            nc.gpsimd.iota(iota_ch[:], [[1, CH]], base=0, channel_multiplier=0,
                           allow_small_or_imprecise_dtypes=True).then_inc(s_const, 1)
            nc.gpsimd.iota(iota_row[:], [[0, 1]], base=0, channel_multiplier=1,
                           allow_small_or_imprecise_dtypes=True).then_inc(s_const, 1)
            nc.gpsimd.memset(ones[:], 1.0).then_inc(s_const, 1)
            nc.gpsimd.memset(eps[:], EPS).then_inc(s_const, 1)
            nc.gpsimd.memset(x_sb[:, NT - 1, :], 0.0).then_inc(s_const, 1)
            nc.gpsimd.memset(zeros16[:], 0.0)
            nc.gpsimd.memset(msg[:, :, D:AW], 1.0).then_inc(s_ones, 1)
            for n, block_ in enumerate((4, 0, 1, 2, 3)):
                if n >= 3:
                    pool.wait_ge(s_wlo, n)
                    pool.dma_start(raw_types, half(Wb, n - 3)).then_inc(s_w[n - 1], 16)
                pool.wait_ge(s_wmax, n + 1)
                nc.gpsimd.partition_all_reduce(wscale[:, block_, 1:2], wscale[:, block_, 0:1], P,
                                               bass.bass_isa.ReduceOp.max).then_inc(s_wall, 1)
            pool.wait_ge(s_clear, 1)
            for n in range(4):
                pool.dma_start(xs_dram.rearrange("(p a) d -> p (a d)", p=P)[:, n * 4096:(n + 1) * 4096],
                               acc[0][:, 0:4096]).then_inc(s_zero_st, 16)
            for d in range(2):
                pool.wait_ge(s_slots, d + 1)
                pool.wait_ge(s_free, 2 + 4 * NT * (d + 1))
                with pool.Fori(0, CH // 16) as i:
                    chain.n = i * 2 + (2 * (CH // 16) * d)
                    for j in range(16):
                        if j % 8 == 0:
                            chain.link(nc.gpsimd.tensor_copy(idx_now[:, j // 8, :], slot_row[d][:, ds(i * 16 + j, 8)]))
                        pool.wait_ge(s_seg, i * 16 + (d * CH + j + SR - MR + 1))
                        pool.sem_inc(s_turn, 1)
                        pool.indirect_dma_start(msg[:, j % MR, 0:D], None, table[d],
                                                bass.IndirectOffsetOnAxis(idx_now[:, j // 8, j % 8:j % 8 + 1], 0)
                                                ).then_inc(s_gath[j % MR], 16)
            pool.wait_ge(s_slot2, 1)
            pool.wait_ge(s_zero_st, 64)
            for n in range(NA):
                t = n % NT
                rows = P if t < NT - 1 else LAST
                if n >= 4:
                    pool.wait_ge(s_scat[n % 4], 16 * (n // 4))
                pool.indirect_dma_start(xs_dram, bass.IndirectOffsetOnAxis(a_slot[0:rows, n:n + 1], 0),
                                        xn2[0:rows, t, :], None).then_inc(s_scat[n % 4], 16)
            for n in range(4):
                pool.wait_ge(s_scat[n], 16 * len(range(n, NA, 4)))
            pool.sem_inc(s_allscat, 1)
            ysv = ys_dram
            pool.sem_inc(s_yf, 2)
            with pool.Fori(0, NST // 2) as i:
                for n in range(2):
                    pool.wait_ge(s_yc, i * 2 + (n + 1))
                    pool.dma_start(ysv[ds((i * 2 + n) * P, P), :], y_sb[n]).then_inc(s_yo[n], 16)
                    pool.wait_ge(s_yo[n], i * 16 + 16)
                    pool.sem_inc(s_yf, 1)
            for t in range(NT):
                rows = P if t < NT - 1 else LAST
                if t >= 4:
                    pool.wait_ge(s_fin, t - 3)
                for c in range(2):
                    pool.indirect_dma_start(y_in[0:rows, 2 * (t % 4) + c, :], None, ys_dram,
                                            bass.IndirectOffsetOnAxis(a_slot[0:rows, c * NT + t:c * NT + t + 1], 0)
                                            ).then_inc(s_yg[t % 4], 16)

        @block.tensor
        def _(pe):
            def sort_chunk(n, j):
                pe.wait_ge(s_ops, n + 1)
                nc.tensor.matmul(sort_ps[0], ops_a[:, j % OR, 0, :], ops_b[:, j % OR, :],
                                 start=False, stop=False, skip_group_check=True)
                nc.tensor.matmul(sort_ps[1], ops_a[:, j % OR, 1, :], ops_b[:, j % OR, :],
                                 start=False, stop=False, skip_group_check=True).then_inc(s_used, 1)

            def sort_open():
                for q in range(2):
                    nc.tensor.matmul(sort_ps[q], zeros16[0:1, :], iota_ch[0:1, :], start=True, stop=False,
                                     skip_group_check=True)

            def sort_close():
                for q in range(2):
                    last = nc.tensor.matmul(sort_ps[q], zeros16[0:1, :], iota_ch[0:1, :], start=False, stop=True,
                                            skip_group_check=True)
                last.then_inc(s_sorted, 1)

            def segment_chunk(n, base, j):
                pe.wait_ge(s_hot, n + 1)
                pe.wait_ge(s_gath[j % MR], base * 32 + 16 * (j // MR + 1))
                pe.wait_ge(s_acc, n + 1)
                nc.tensor.matmul(seg_ps[j % 2], onehot[:, j % SR, :], msg[:, j % MR, :],
                                 start=True, stop=True).then_inc(s_seg, 1)

            def project(i, d, b):
                h, q = b // 4, b % 4
                pe.wait_ge(s_evac, i * 8 + (d * NT * 8 + b + 1))
                parts = [(k, f, w) for k in range(KD) for f, w in ((f_hi, w_hi), (f_hi, w_lo), (f_lo, w_hi))]
                for n, (k, f, w) in enumerate(parts):
                    moving = w[:, d, h * WH:(h + 1) * WH].rearrange("p (t k o) -> p t k o", k=KD, o=D)[
                        :, 2 * q:2 * q + 2, k, :]
                    last = nc.tensor.matmul(ps[:, q, :], f[:, k, ds(i * P, P)], moving,
                                            start=(n == 0), stop=(n == len(parts) - 1))
                last.then_inc(s_proj, 1)

            pe.wait_ge(s_const, 10)
            pe.wait_ge(s_ones, 1)
            pe.sem_inc(s_flo, 5)
            with pe.Fori(0, 5) as i:
                for j in range(5):
                    pe.wait_ge(s_xn, i * 5 + (j + 1))
                    pe.wait_ge(s_flo, i * 5 + (j + 1))
                    for k in range(KD):
                        last = nc.tensor.transpose(ps[:, j, k * P:(k + 1) * P], xn[:, j, k::KD], ident[:])
                    last.then_inc(s_xt, 1)
            pe.wait_ge(s_flo, NT + 5)
            pe.wait_ge(s_wlo, 1)
            pe.sem_inc(s_base, 5)
            with pe.Fori(0, 5) as i:
                for j in range(5):
                    pe.wait_ge(s_base, i * 5 + (j + 1))
                    parts = [(k, f, w) for k in range(KD) for f, w in ((f_hi, loop_hi), (f_hi, loop_lo), (f_lo, loop_hi))]
                    for n, (k, f, w) in enumerate(parts):
                        last = nc.tensor.matmul(ps[:, j, 0:D], f[:, k, ds((i * 5 + j) * P, P)],
                                                w[:, k * D:(k + 1) * D], start=(n == 0), stop=(n == len(parts) - 1))
                    last.then_inc(s_loop, 1)
            def rank_products(cnt, rows, groups, chunks, n):
                pe.wait_ge(s_cnt, n + 1)
                nc.tensor.matmul(rank_ps[:, 0:groups], before[0:rows, :], cnt, start=True, stop=True)
                nc.tensor.matmul(rank_ps[:, 32:32 + groups], ones[0:rows, :], cnt, start=True, stop=True)
                nc.tensor.matmul(rank_ps[0:groups, 64:65], cnt, ones[0:rows, 0:1], start=True, stop=True).then_inc(s_tot, 1)
                pe.wait_ge(s_inc, n + 1)
                nc.tensor.matmul(rank_ps[0:groups, 65:66], upto[0:groups, 0:groups], small[0:groups, 8, 0:1],
                                 start=True, stop=True).then_inc(s_incp, 1)
                pe.wait_ge(s_cmp, n + 1)
                nc.tensor.matmul(ps[0:1, 7, 0:chunks], ones[0:groups, 0:1], onehot_flat[0:groups, 0:chunks],
                                 start=True, stop=True).then_inc(s_map, 1)

            pe.wait_ge(s_base, NT + 5)
            for d in range(2):
                rank_products(small[0:EP, 0, 0:NT], EP, NT, CH, d)
            pe.wait_ge(s_wlo, 3)
            with pe.Fori(0, PRE) as i:
                for b in range(8):
                    project(i, 0, b)
            pe.sem_inc(s_used, OR)
            sort_open()
            with pe.Fori(0, NT - PRE) as i:
                for b in range(8):
                    project(i + PRE, 0, b)
                    for j in range(b * A_SORT // 8, (b + 1) * A_SORT // 8):
                        sort_chunk(i * A_SORT + j, j)
            sort_close()
            pe.wait_ge(s_wlo, 5)
            pe.wait_ge(s_slots, 1)
            sort_open()
            pe.sem_inc(s_seg, SR)
            with pe.Fori(0, NT) as i:
                for b in range(8):
                    project(i, 1, b)
                    for j in range(b * B_SORT // 8, (b + 1) * B_SORT // 8):
                        sort_chunk(i * B_SORT + (EC + j), j)
                    for j in range(2 * b, 2 * b + 2):
                        segment_chunk(i * 16 + j, i, j)
            sort_close()
            for j in range(16):
                segment_chunk(NT * 16 + j, NT, j)
            with pe.Fori(0, CH // 16) as i:
                for j in range(16):
                    segment_chunk(i * 16 + (CH + j), i + CH // 16, j)
            for t in range(NT + 1):
                if t < NT:
                    pe.wait_ge(s_x1, t + 1)
                    pe.wait_ge(s_x2c, t + 1)
                    for k in range(KD):
                        last = nc.tensor.transpose(ps[:, t % 4, k * P:(k + 1) * P], xn2[:, t, k::KD], ident[:])
                    last.then_inc(s_x2t, 1)
                if t >= 1:
                    pe.wait_ge(s_x2c, t + 4)
                    for k in range(KD):
                        last = nc.tensor.matmul(ps[:, 4, (t - 1) * NE:t * NE], xn2_t[:, (t - 1) % 4, k, :], gw[:, k, :],
                                                start=(k == 0), stop=(k == KD - 1))
            last.then_inc(s_gate, 1)
            rank_products(small[:, 0, 0:NE], P, NE, NST, 2)
            pe.wait_ge(s_map, 3)
            pe.sem_inc(s_y, 2)

            def slot_transpose(n, j):
                pe.wait_ge(s_xsin[j], n * 16 + 16)
                for k in range(KD):
                    last = nc.tensor.transpose(ps[:, j, k * P:(k + 1) * P], xs_in[j][:, k::KD], ident[:])
                last.then_inc(s_mt, 1)

            with pe.Fori(0, NST // 2) as i:
                for n in range(2):
                    slot_transpose(i, n)
                    pe.wait_ge(s_mtc, i * 2 + (n + 1))
                    pe.wait_ge(s_ew[n], i * 48 + 48)
                    for q, w in ((0, ew1[n]), (1, ew2[n])):
                        for c in range(KH):
                            for k in range(KD):
                                last = nc.tensor.matmul(ps[:, 2 + 2 * n + q, c * P:(c + 1) * P], w[:, k, c::KH],
                                                        xs_t[n][:, k, :], start=(k == 0), stop=(k == KD - 1))
                    last.then_inc(s_h, 1)
                    pe.wait_ge(s_hm, i * 2 + (n + 3))
                    for c in range(KH):
                        last = nc.tensor.matmul(ps[:, 6 + n, 0:D], h_out[n][:, c, :], ew3[n][:, c, :],
                                                start=(c == 0), stop=(c == KH - 1))
                    last.then_inc(s_y, 1)

        @block.vector
        def _(dve):
            v = nc.vector
            chain = Chain(dve, s_dve)
            mark, link = chain.mark, chain.link

            def fence():
                link(v.memset(fence_cell[:], 0.0))

            def layernorm_stats(nth):
                me, mo = stats[:, :, 1], stats[:, :, 4]
                fence()
                link(v.tensor_tensor(st[:, 3], me, mo, ALU.add))
                link(v.tensor_tensor(st[:, 4], me, mo, ALU.subtract))
                mark(v.tensor_scalar(mean, st[:, 3], 0.5, None, ALU.mult))
                link(v.scalar_tensor_tensor(st[:, 5], st[:, 4], 0.25, st[:, 4], ALU.mult, ALU.mult))
                link(v.tensor_tensor(st[:, 3], stats[:, :, 2], stats[:, :, 5], ALU.add))
                v.scalar_tensor_tensor(st[:, 2], st[:, 3], 1.0 / D, st[:, 5], ALU.mult, ALU.add).then_inc(s_var, 1)
                dve.wait_ge(s_std, nth)
                link(v.reciprocal(rstd, st[:, 1]))

            def weight_max(raw, block_):
                v.tensor_reduce(wscale[:, block_, 0:1], raw, AX.X, ALU.max,
                                apply_absolute_value=True).then_inc(s_wmax, 1)

            def weight_scale(block_, nth):
                dve.wait_ge(s_wall, nth)
                link(v.tensor_scalar(wscale[:, block_, 1:2], wscale[:, block_, 1:2], 1e-30, None, ALU.max))
                link(v.tensor_scalar(wscale[:, block_, 2:3].bitcast(i32), wscale[:, block_, 1:2].bitcast(i32),
                                     EXP_MASK, None, ALU.bitwise_and))
                v.tensor_scalar(wscale[:, block_, 3:4].bitcast(i32), wscale[:, block_, 2:3].bitcast(i32), -1.0,
                                EXP_TWICE_BIAS, ALU.mult, ALU.add).then_inc(s_wsc, 1)
                dve.wait_ge(s_wsc, nth)

            def weight_low(lo, hi, raw, block_, nth):
                dve.wait_ge(s_whi, nth)
                v.scalar_tensor_tensor(lo, raw, wscale[:, block_, 3:4], hi, ALU.mult, ALU.subtract).then_inc(s_wlo, 1)

            dve.wait_ge(s_const, 6)
            v.tensor_scalar(ident[:], iota_p[:], iota_row[:], None, ALU.is_equal)
            v.tensor_scalar(before[:], iota_p[:], iota_row[:], None, ALU.is_gt).then_inc(s_const, 1)
            v.tensor_scalar(upto[:], iota_p[:], iota_row[:], None, ALU.is_ge)
            v.tensor_copy(iota_p16[:], iota_p[:])
            v.memset(valid[:], 1.0).then_inc(s_dve, 1)
            chain.n = 1
            dve.wait_ge(s_dve, 1)
            mark(v.tensor_scalar(valid[:, NT - 1:NT], iota_row[:], float(LAST), None, ALU.is_lt))
            v.memset(small[:], 0.0).then_inc(s_const, 3)
            dve.wait_ge(s_x, 16)
            dve.wait_ge(s_xl, 16)
            with dve.Fori(0, NT) as t:
                v.bn_stats(stats[:, ds(t, 1), :].rearrange("p a b -> p (a b)"),
                           x_sb[:, ds(t, 1), :].rearrange("p a b -> p (a b)"))
            layernorm_stats(1)
            dve.wait_ge(s_lw, 16)
            weight_max(loop_raw, 4)
            weight_scale(4, 1)
            weight_low(loop_lo[:], loop_hi[:], loop_raw, 4, 1)
            with dve.Fori(0, 5) as i:
                for j in range(5):
                    t = i * 5 + j
                    v.tensor_scalar(xn[:, j, :], x_sb[:, ds(t, 1), :].rearrange("p a b -> p (a b)"),
                                    st[:, 0, ds(t, 1)], st[:, 1, ds(t, 1)], ALU.subtract, ALU.mult).then_inc(s_xn, 1)
                for j in range(5):
                    t = i * 5 + j
                    dve.wait_ge(s_fhi, t + 1)
                    v.tensor_tensor(f_lo[:, :, ds(t * P, P)], ps[:, j, 0:D].rearrange("p (k n) -> p k n", k=KD),
                                    f_hi[:, :, ds(t * P, P)], ALU.subtract).then_inc(s_flo, 1)
            def forward_weights(n):
                dve.wait_ge(s_w[n], 16)
                weight_max(w_raw, n)
                weight_scale(n, n + 2)
                weight_low(w_lo[:, 0, n * WH:(n + 1) * WH], w_hi[:, 0, n * WH:(n + 1) * WH], w_raw, n, n + 2)

            forward_weights(0)
            dve.wait_ge(s_rows, 80)
            link(v.tensor_scalar(wscale[:, 4, 0:1], wscale[:, 4, 2:3], 2.0, None, ALU.mult))
            n0 = chain.n
            with dve.Fori(0, 5) as i:
                chain.n = i * 5 + n0
                for j in range(5):
                    xt = x_sb[:, ds(i * 5 + j, 1), :].rearrange("p a b -> p (a b)")
                    dve.wait_ge(s_loop, i * 5 + (j + 1))
                    link(v.scalar_tensor_tensor(xt, ps[:, j, 0:D], wscale[:, 4, 0:1], xt, ALU.mult, ALU.add))
                    v.tensor_tensor(xt, xt, bias_s, ALU.add).then_inc(s_base, 1)
            chain.n = n0 + NT
            forward_weights(1)

            def group_ends(groups, n):
                g = slice(0, groups)
                dve.wait_ge(s_tot, n + 1)
                mark(v.tensor_copy(small[:, 1, g], rank_ps[:, 0:groups]))
                mark(v.tensor_scalar(small_i[:, 0, g], rank_ps[:, 32:32 + groups], float(P - 1), None, ALU.add))
                link(v.tensor_scalar(small_i[0:groups, 1, 0:1], rank_ps[0:groups, 64:65], float(P - 1), None, ALU.add))
                link(v.tensor_scalar(small_i[:, 0, g], small_i[:, 0, g], 7, None, ALU.arith_shift_right))
                link(v.tensor_scalar(small_i[0:groups, 1, 0:1], small_i[0:groups, 1, 0:1], 7, None,
                                     ALU.arith_shift_right))
                mark(v.tensor_copy(small[:, 2, g], small_i[:, 0, g]))
                v.tensor_copy(small[0:groups, 8, 0:1], small_i[0:groups, 1, 0:1]).then_inc(s_inc, 1)
                dve.wait_ge(s_inc, n + 1)
                link(v.tensor_tensor_scan(small[:, 3, g], small[:, 2, g], small[:, 2, g], 0.0, ALU.add, ALU.max))
                link(v.tensor_tensor(small[:, 4, g], small[:, 3, g], small[:, 2, g], ALU.subtract))
                link(v.scalar_tensor_tensor(small[:, 5, g], small[:, 4, g], float(P), small[:, 1, g],
                                            ALU.mult, ALU.add))

            def chunk_map(groups, chunks, n, out_i, scale, last_group):
                dve.wait_ge(s_incp, n + 1)
                link(v.tensor_copy(small[0:groups, 9, 0:1], rank_ps[0:groups, 65:66]))
                v.tensor_scalar(onehot_flat[0:groups, 0:chunks], iota_ch[0:groups, 0:chunks],
                                small[0:groups, 9, 0:1], None, ALU.is_ge).then_inc(s_cmp, 1)
                dve.wait_ge(s_map, n + 1)
                link(v.tensor_scalar(out_i, ps[0:1, 7, 0:chunks], float(last_group), float(scale), ALU.min, ALU.mult))

            dve.wait_ge(s_edges, 48)
            for d, (target, source) in enumerate(((e_dst, e_src), (e_src, e_dst))):
                link(v.tensor_scalar(e_int, target, 7, None, ALU.arith_shift_right))
                mark(v.tensor_copy(e_key, e_int))
                mark(v.tensor_scalar(pay_2[d], source, -SRC_BIAS, None, ALU.add))
                link(v.scalar_tensor_tensor(e_scan, e_int, -float(P), target, ALU.mult, ALU.add))
                link(v.scalar_tensor_tensor(e_pos, e_typ, float(P), e_scan, ALU.mult, ALU.add))
                mark(v.tensor_scalar(pay_1[d], e_pos, 1.0, None, ALU.add))
                n0 = chain.n
                with dve.Fori(0, NT) as g:
                    chain.n = g + n0
                    link(v.tensor_scalar(e_eq[:, 0, :], e_key, iota_p[0:EP, ds(g, 1)], None, ALU.is_equal, ALU.add,
                                         accum_out=small[0:EP, 0, ds(g, 1)]))
                chain.n = n0 + NT
                dve.sem_inc(s_cnt, 1)
                group_ends(NT, d)
                chunk_map(NT, CH, d, tile_at[d][:], AW, NT - 1)
                link(v.tensor_scalar(e_eq[:, 0, :], e_key, 0.0, None, ALU.is_equal))
                link(v.tensor_tensor_scan(e_scan, e_eq[:, 0, :], e_eq[:, 0, :], small[0:EP, 5, 0:1], ALU.add, ALU.max))
                n0 = chain.n
                with dve.Fori(0, NT // 2) as g2:
                    chain.n = g2 * 6 + n0
                    for q in range(2):
                        g = g2 * 2 + q
                        mark(v.tensor_scalar(e_eq[:, 1 - q, :], e_key, iota_p[0:EP, ds(g + 1, 1)], None, ALU.is_equal))
                        mark(v.copy_predicated(e_pos, e_eq[:, q, :].bitcast(u16), e_scan))
                        dve.wait_ge(s_dve, chain.n)
                        link(v.tensor_tensor_scan(e_scan, e_eq[:, 1 - q, :], e_eq[:, 1 - q, :],
                                                  small[0:EP, 5, ds(g + 1, 1)], ALU.add, ALU.max))
                chain.n = n0 + (NT // 2) * 6
                link(v.copy_predicated(e_pos, e_eq[:, 0, :].bitcast(u16), e_scan))
                link(v.tensor_scalar(e_int, e_pos, -1.0, None, ALU.add))
                link(v.tensor_copy(e_scan, e_int))
                link(v.tensor_scalar(e_int, e_int, 7, None, ALU.arith_shift_right))
                link(v.tensor_copy(pos_b[d], e_int))
                link(v.scalar_tensor_tensor(pos_a[d], pos_b[d], -float(P), e_scan, ALU.mult, ALU.add))
            for n in range(2, 4):
                dve.wait_ge(s_w[n], 16)
                weight_max(w_raw, n)
                weight_scale(n, n + 2)
                hi = w_hi[:, 1, (n - 2) * WH:(n - 1) * WH]
                v.tensor_scalar(hi, w_raw, wscale[:, n, 3:4], None, ALU.mult).then_inc(s_whi, 1)
                weight_low(w_lo[:, 1, (n - 2) * WH:(n - 1) * WH], hi, w_raw, n, n + 2)
            dve.wait_ge(s_wlo, 5)
            v.memset(acc[0][:], 0.0).then_inc(s_clear, 1)

            def sort_operands(d, n, col, j):
                dve.wait_ge(s_used, n + 1)
                v.tensor_scalar(ops_b[:, j % OR, :], iota_ch[0:EP, :], pos_b[d][:, ds(col, 1)], None, ALU.is_equal)
                v.tensor_scalar(ops_a[:, j % OR, 0, :], iota_p16[0:EP, :], pos_a[d][:, ds(col, 1)],
                                pay_1[d][:, ds(col, 1)], ALU.is_equal, ALU.mult)
                v.tensor_scalar(ops_a[:, j % OR, 1, :], iota_p16[0:EP, :], pos_a[d][:, ds(col, 1)],
                                pay_2[d][:, ds(col, 1)], ALU.is_equal, ALU.mult).then_inc(s_ops, 1)

            def slot_tables(d):
                tmp = onehot_flat
                dve.wait_ge(s_sorted, d + 1)
                mark(v.tensor_scalar(tmp[:, 0:CH], sort_ps[0], -1.0, None, ALU.add))
                link(v.tensor_scalar(tmp[:, CH:2 * CH].bitcast(i32), sort_ps[0], -1.0, 0.0, ALU.add, ALU.max))
                link(v.tensor_scalar(tmp[:, CH:2 * CH].bitcast(i32), tmp[:, CH:2 * CH].bitcast(i32), 7, None,
                                     ALU.arith_shift_right))
                mark(v.scalar_tensor_tensor(slot_loc[d][:], tmp[:, CH:2 * CH].bitcast(i32), -float(P), tmp[:, 0:CH],
                                            ALU.mult, ALU.add))
                dve.wait_ge(s_dve, chain.n)
                link(v.tensor_scalar(tmp[:, 0:CH], sort_ps[1], SRC_BIAS, float(R), ALU.add, ALU.mult))
                mark(v.tensor_tensor(slot_row[d][:], tmp[:, 0:CH], tmp[:, CH:2 * CH].bitcast(i32), ALU.add))
                dve.wait_ge(s_dve, chain.n)
                dve.sem_inc(s_slots, 1)

            tile_regs = [dve.alloc_register(f"tile_reg_{q}") for q in range(4)]

            def onehot_chunk(d, n, col, j):
                dve.wait_ge(s_seg, n + 1)
                v.tensor_scalar(onehot[:, j % SR, :], iota_p[:], slot_loc[d][:, ds(col, 1)], None,
                                ALU.is_equal).then_inc(s_hot, 1)

            def load_tiles(d, col):
                dve.load(tile_regs, tile_at[d][0:1, ds(col, 4)])
                return [dve.snap(r, min_val=0, max_val=(NT - 1) * AW) for r in tile_regs]

            def add_chunk(d, n, j, at):
                dve.wait_ge(s_seg, n + (SR + 1))
                dve.wait_ge(s_acc, n + 2)
                a = acc[d][:, ds(at, AW)]
                v.tensor_tensor(a, a, seg_ps[j % 2], ALU.add).then_inc(s_acc, 1)

            def sums_turn(d, i, more, sort):
                for j0 in range(0, 16, 2):
                    for j in (j0, j0 + 1):
                        if sort:
                            sort_operands(1, i * B_SORT + (EC + j), i * B_SORT + j, j)
                    for j in (j0, j0 + 1):
                        if more or j < 16 - LEAD:
                            onehot_chunk(d, i * 16 + (d * CH + j + LEAD), i * 16 + (j + LEAD), j + LEAD)
                    if j0 % 4 == 0:
                        at = load_tiles(d, i * 16 + j0)
                    for j in (j0, j0 + 1):
                        add_chunk(d, i * 16 + (d * CH + j), j, at[j % 4])

            with dve.Fori(0, EC // OR) as i:
                for j in range(OR):
                    sort_operands(0, i * OR + j, i * OR + j, j)
            slot_tables(0)
            dve.wait_ge(s_zero_st, 64)
            dve.sem_inc(s_acc, 2)
            dve.wait_ge(s_slots, 1)
            for j in range(LEAD):
                onehot_chunk(0, j, j, j)
            with dve.Fori(0, NT) as i:
                sums_turn(0, i, True, True)
            sums_turn(0, NT, False, False)
            dve.wait_ge(s_seg, CH + SR)
            slot_tables(1)
            link(v.memset(acc[1][:], 0.0))
            for j in range(LEAD):
                onehot_chunk(1, CH + j, j, j)
            with dve.Fori(0, CH // 16 - 1) as i:
                sums_turn(1, i, True, False)
            sums_turn(1, CH // 16 - 1, False, False)
            dve.wait_ge(s_acc, 2 * CH + 2)
            for d in range(2):
                deg = acc[d][:, :].rearrange("p (t a) -> p t a", a=AW)[:, :, D]
                link(v.tensor_scalar(small[:, 2 * d, 0:NT], deg, 1.0, None, ALU.max))
                mark(v.tensor_scalar(small[:, 2 * d + 1, 0:NT], deg, 1.0, None, ALU.min))
                link(v.reciprocal(small[:, 2 * d, 0:NT], small[:, 2 * d, 0:NT]))
            n0 = chain.n
            with dve.Fori(0, NT) as t:
                chain.n = t * 4 + n0
                xt = x_sb[:, ds(t, 1), :].rearrange("p a b -> p (a b)")
                for d, bias in enumerate((bias_f, bias_b)):
                    link(v.scalar_tensor_tensor(xt, acc[d][:, ds(t * AW, D)], small[:, 2 * d, ds(t, 1)], xt,
                                                ALU.mult, ALU.add))
                    link(v.scalar_tensor_tensor(xt, bias[:], small[:, 2 * d + 1, ds(t, 1)], xt, ALU.mult, ALU.add))
                v.bn_stats(stats[:, ds(t, 1), :].rearrange("p a b -> p (a b)"), xt)
            chain.n = n0 + 4 * NT
            link(v.memset(small[:], 0.0))
            layernorm_stats(2)
            with dve.Fori(0, NT) as t:
                v.tensor_scalar(xn2[:, ds(t, 1), :].rearrange("p a b -> p (a b)"),
                                x_sb[:, ds(t, 1), :].rearrange("p a b -> p (a b)"),
                                st[:, 0, ds(t, 1)], st[:, 1, ds(t, 1)], ALU.subtract, ALU.mult).then_inc(s_x1, 1)
            def over_e(a):
                return a.unsqueeze(2).to_broadcast([P, NT, NE])

            dve.wait_ge(s_gate, 1)
            link(v.tensor_tensor(gate[0], ps[:, 4, 0:NT * NE].rearrange("p (t e) -> p t e", e=NE),
                                 gb[:, :].unsqueeze(1).to_broadcast([P, NT, NE]), ALU.add))
            link(v.tensor_reduce(prob[0], gate[0], AX.X, ALU.max))
            v.tensor_tensor(gate[1], gate[0], over_e(prob[0]), ALU.subtract).then_inc(s_sub, 1)
            dve.wait_ge(s_exp, 1)
            link(v.tensor_reduce(prob[1], gate[2], AX.X, ALU.add))
            link(v.reciprocal(prob[1], prob[1]))
            link(v.tensor_tensor(gate[0], gate[2], over_e(prob[1]), ALU.mult))
            link(v.tensor_scalar(small[:, 6, 0:NE], iota_p[:, 0:NE], -1.0, float(NE), ALU.mult, ALU.add))
            rank_e = small[:, 6, 0:NE].unsqueeze(1).to_broadcast([P, NT, NE])
            pick = assign.rearrange("p e (c t) -> p c t e", c=2)
            for c in range(2):
                link(v.tensor_reduce(prob[2 + c], gate[0], AX.X, ALU.max))
                link(v.tensor_tensor(gate[1], gate[0], over_e(prob[2 + c]), ALU.is_equal))
                link(v.tensor_tensor(gate[2], gate[1], rank_e, ALU.mult))
                link(v.tensor_reduce(prob[4], gate[2], AX.X, ALU.max))
                link(v.tensor_tensor(gate[3], gate[2], over_e(prob[4]), ALU.is_equal))
                link(v.scalar_tensor_tensor(gate[0], gate[3], -2.0, gate[0], ALU.mult, ALU.add))
                link(v.tensor_tensor(pick[:, c], gate[3], over_e(valid[:]), ALU.mult))
            link(v.tensor_tensor(prob[4], prob[2], prob[3], ALU.add))
            link(v.reciprocal(prob[5], prob[4]))
            link(v.tensor_tensor(prob[2], prob[2], prob[5], ALU.mult))
            link(v.tensor_tensor(prob[3], prob[3], prob[5], ALU.mult))
            flat = assign.rearrange("p e j -> p (e j)")
            link(v.tensor_tensor_scan(a_scan.rearrange("p e j -> p (e j)"), flat, flat, 0.0, ALU.add, ALU.max))
            ends = a_scan[:, :, NA - 1]
            link(v.tensor_copy(small[:, 7, 1:NE], ends[:, 0:NE - 1]))
            v.tensor_tensor(small[:, 0, 0:NE], ends, small[:, 7, 0:NE], ALU.subtract).then_inc(s_cnt, 1)
            group_ends(NE, 2)
            chunk_map(NE, NST, 2, expert_at[:], 1, NE - 1)
            link(v.tensor_tensor(small[:, 5, 0:NE], small[:, 5, 0:NE], small[:, 7, 0:NE], ALU.subtract))
            link(v.tensor_tensor(a_scan, a_scan, small[:, 5, 0:NE].unsqueeze(2).to_broadcast([P, NE, NA]), ALU.add))
            link(v.tensor_tensor(a_scan, a_scan, assign, ALU.mult))
            link(v.tensor_reduce(a_pos, a_scan.rearrange("p e j -> p j e"), AX.X, ALU.add))
            v.tensor_scalar(a_slot, a_pos, -1.0, 0.0, ALU.add, ALU.max).then_inc(s_slot2, 1)
            dve.sem_inc(s_hm, 2)
            with dve.Fori(0, NST // 2) as i:
                for n in range(2):
                    dve.wait_ge(s_mt, i * 2 + (n + 1))
                    v.tensor_copy(xs_t[n], ps[:, n, 0:D].rearrange("p (k s) -> p k s", k=KD)).then_inc(s_mtc, 1)
                    dve.wait_ge(s_silu, i * 2 + (n + 1))
                    v.tensor_tensor(h_out[n], h_act[n].rearrange("p (c s) -> p c s", c=KH),
                                    ps[:, 3 + 2 * n, :].rearrange("p (c s) -> p c s", c=KH), ALU.mult).then_inc(s_hm, 1)
            for t in range(NT):
                dve.wait_ge(s_yg[t % 4], 32 * (t // 4 + 1))
                link(v.scalar_tensor_tensor(x_sb[:, t, :], y_in[:, 2 * (t % 4), :], prob[2][:, t:t + 1], x_sb[:, t, :],
                                            ALU.mult, ALU.add))
                v.scalar_tensor_tensor(x_sb[:, t, :], y_in[:, 2 * (t % 4) + 1, :], prob[3][:, t:t + 1], x_sb[:, t, :],
                                       ALU.mult, ALU.add).then_inc(s_fin, 1)


_INS = ['x', 'src', 'dst', 'edge_type_16', 'L0_gnn_Wf', 'L0_gnn_Wb', 'L0_gnn_loop_weight', 'L0_gnn_forward_bias',
        'L0_gnn_backward_bias', 'L0_gnn_self_bias', 'L0_ffn_gate_w', 'L0_ffn_gate_b', 'L0_ffn_w1', 'L0_ffn_w2',
        'L0_ffn_w3']


def kernel(**inputs):
    import numpy as _np
    import concourse.bacc as _bacc
    from concourse import mybir as _mybir
    from concourse.bass_utils import run_bass_kernel_spmd as _run

    nc = _bacc.Bacc("TRN2", target_bir_lowering=False, num_devices=1)
    arrays, args = {}, []
    for name in _INS:
        a = _np.ascontiguousarray(inputs[name])
        arrays[f"in_{name}"] = a
        args.append(nc.dram_tensor(f"in_{name}", a.shape, _mybir.dt.from_np(a.dtype), kind="ExternalInput").ap())
    args.append(nc.dram_tensor("out_0", (N, D), fp32, kind="ExternalOutput").ap())
    build(nc, *args)
    r = _run(nc, [arrays], core_ids=[0])
    return r.results[0]["out_0"]
```

```python
import concourse.bass as bass
from concourse import mybir
from contextlib import ExitStack

fp32 = mybir.dt.float32
f16 = mybir.dt.float16
i32 = mybir.dt.int32
i16 = mybir.dt.int16
u16 = mybir.dt.uint16
ALU = mybir.AluOpType
ACT = mybir.ActivationFunctionType
AX = mybir.AxisListType
ds = bass.ds

P = 128
N = 3125
D = 256
KD = D // P
NT = (N + P - 1) // P
LAST = N - (NT - 1) * P
R = 16
E = 50000
EP, EC = 125, 400
assert EP * EC == E
CH = 416
assert CH >= (E + NT * (P - 1)) // P and CH % 16 == 0
AW = D + 2
HALF = R // 2
WH = HALF * KD * D
NS = 4
MR = 8
SR = 8
OR = (5, 4)
LEAD = 4
PRE0 = 3
PRE = 9
A_SORT = EC // (NT - PRE)
B_SORT = EC // NT
NE = 16
H = 512
KH = H // P
NST = (2 * N + NE * (P - 1)) // P
NA = 2 * NT
EW = 3 * KD * H
ER = 2 * EW + 16
EPS = 1e-5
SRC_BIAS = 1562.0
EXP_MASK = 0x7F800000
EXP_TWICE_BIAS = float(0x7F000000)


class Chain:

    def __init__(self, eng, sem):
        self.eng, self.sem, self.n = eng, sem, 0

    def mark(self, ins):
        ins.then_inc(self.sem, 1)
        self.n = self.n + 1

    def link(self, ins):
        self.mark(ins)
        self.eng.wait_ge(self.sem, self.n)


def build(nc, x, src, dst, typ, Wf, Wb, loopw, fbias, bbias, sbias, gate_w, gate_b, w1, w2, w3, out):
    ctx = ExitStack()
    with ctx:
        def sb(name, shape, dt=fp32):
            return ctx.enter_context(nc.sbuf_tensor(name, shape, dt))

        def sem(name):
            return ctx.enter_context(nc.semaphore(name))

        table = [nc.dram_tensor("messages_fwd", (NT * P * R, 2 * D), f16).ap(),
                 nc.dram_tensor("messages_bwd", (NT * P * R, D), fp32).ap()]
        xs_dram = nc.dram_tensor("slot_rows", (NST * P, D), fp32).ap()
        ys_dram = nc.dram_tensor("slot_results", (NST * P, D), fp32).ap()
        ew_dram = nc.dram_tensor("expert_parts", (NE * P, ER), f16).ap()

        x_sb = sb("x_sb", [P, NT, D])
        acc = [sb("acc_f", [P, NT * AW]), sb("acc_b", [P, NT * AW])]
        SUM0, DEG = (0, 1), (D, 0)
        f_hi = sb("f_hi", [P, KD, NT * P], f16)
        f_lo = sb("f_lo", [P, KD, NT * P], f16)
        w_hi = sb("w_hi", [P, 2, 2 * WH], f16)
        w_lo = sb("w_lo", [P, 2, 2 * WH], f16)
        stage = sb("stage", [P, NS, 2 * D])
        msg = sb("msg", [P, MR, AW])
        onehot = sb("onehot", [P, SR, P])
        ops_b_4 = sb("ops_b", [EP, 4, CH], f16)
        ops_a_4 = sb("ops_a", [EP, 4, 2, P], f16)
        slot_row = [sb(f"slot_row_{n}", [P, CH], i32) for n in "fb"]
        slot_loc = [sb(f"slot_loc_{n}", [P, CH], f16) for n in "fb"]
        tile_at = [sb(f"tile_at_{n}", [1, CH], i16) for n in "fb"]
        idx_now = sb("idx_now", [P, 2, 8], i32)
        iota_ch = sb("iota_ch", [P, CH], f16)
        iota_p = sb("iota_p", [P, P])
        iota_p16 = sb("iota_p16", [P, P], f16)
        iota_row = sb("iota_row", [P, 1])
        ident = sb("ident", [P, P])
        minus16 = sb("minus16", [P, P], f16)
        before = sb("before", [P, P], f16)
        upto = sb("upto", [P, 32])
        ones = sb("ones", [P, P])
        ones16 = sb("ones16", [P, P], f16)
        zeros16 = sb("zeros16", [1, P], f16)
        loop_hi = sb("loop_hi", [P, KD * D], f16)
        loop_lo = sb("loop_lo", [P, KD * D], f16)
        bias_f = sb("bias_f", [P, D])
        bias_b = sb("bias_b", [P, D])
        gw = sb("gw", [P, KD, NE])
        gb = sb("gb", [P, NE])
        eps = sb("eps", [P, 1])
        wscale = sb("wscale", [P, 3, 6])
        stats = sb("stats", [P, NT, 6])
        st = sb("st", [P, 6, NT])
        mean, rstd = st[:, 0], st[:, 1]
        small = sb("small", [P, 12, 32])
        small_i = sb("small_i", [P, 2, 32], i32)
        cnt16 = sb("cnt16", [P, 32], f16)
        valid = sb("valid", [P, NT])
        fence_cell = sb("fence_cell", [1, 1])
        expert_at = sb("expert_at", [1, NST], i32)

        stage16 = stage[:, :, :].rearrange("p s c -> p (s c)").bitcast(f16).rearrange(
            "p (s t h o) -> p s t h o", s=NS, t=2, h=2)
        msg16 = msg[:, :, :].rearrange("p s c -> p (s c)").bitcast(f16).rearrange("p (s c) -> p s c", s=MR)
        onehot_flat = onehot[:, :, :].rearrange("p a b -> p (a b)")
        onehot16 = onehot_flat.bitcast(f16).rearrange("p (a b) -> p a b", a=SR)

        flat16 = onehot_flat.bitcast(f16)
        ops_b = [ops_b_4[:, j, :] for j in range(4)] + [flat16[0:EP, 0:CH]]
        ops_a = [ops_a_4[:, j] for j in range(4)] + [
            flat16[0:EP, CH:CH + 2 * P].rearrange("p (a b) -> p a b", a=2)]
        w_raw = [acc[0][:, 0:WH], acc[1][:, 0:WH]]
        loop_raw = acc[0][:, WH:WH + KD * D]
        xn = acc[0][:, WH + KD * D:WH + KD * D + 5 * D].rearrange("p (j d) -> p j d", j=5)
        bias_s = acc[0][:, WH + (KD + 5) * D:WH + (KD + 6) * D]

        def edge(k):
            return acc[1][0:EP, k * EC:(k + 1) * EC]
        pos_b, pos_a = [edge(0), edge(4)], [edge(1), edge(5)]
        pay_1, pay_2 = [edge(2), edge(6)], [edge(3), edge(7)]
        e_src, e_dst, e_typ = edge(8).bitcast(i32), edge(9).bitcast(i32), edge(10).bitcast(i32)
        e_int, e_scan, e_pos = edge(11).bitcast(i32), edge(12), edge(13)
        e_key = edge(14).bitcast(f16).rearrange("p (a b) -> p a b", a=2)
        e_eq = edge(15).bitcast(f16).rearrange("p (a b) -> p a b", a=2)
        assert 16 * EC <= NT * AW
        fbuf = f_hi[:, :, :].rearrange("p k n -> p (k n)")
        wh_flat = w_hi[:, :, :].rearrange("p a b -> p (a b)")
        wl_flat = w_lo[:, :, :].rearrange("p a b -> p (a b)")
        e_raw = [fbuf.bitcast(fp32)[:, 0:EW], wl_flat[:, 2 * EW:4 * EW].bitcast(fp32)]
        parts = [wh_flat[:, 0:ER], wh_flat[:, ER:2 * ER]]
        assert 2 * ER <= 4 * WH and 4 * EW <= 4 * WH

        def factor(n, k):
            return parts[n][:, 2 * EW:2 * EW + 16].bitcast(fp32)[:, k:k + 1]

        def matrix(n, low, m):
            return parts[n][:, low * EW + m * KD * H:low * EW + (m + 1) * KD * H]
        emax = sb("emax", [P, 12])
        escale = sb("escale", [P, 8])
        parts.extend(acc[0][:, n * ER // 2:(n + 1) * ER // 2].bitcast(f16) for n in range(2))
        assert ER <= NT * AW
        wbase2 = wl_flat[:, 0:2 * EW].bitcast(fp32)
        xs_in = [wbase2[:, n * D:(n + 1) * D] for n in range(2)]
        h_act = [wbase2[:, (2 + 2 * n) * D:(4 + 2 * n) * D] for n in range(2)]
        y_sb = [wbase2[:, (6 + n) * D:(7 + n) * D] for n in range(4)]
        xs_t = [wl_flat[:, (20 + 2 * n) * D:(22 + 2 * n) * D].rearrange("p (a k s) -> p a k s", a=2, k=KD) for n in range(2)]
        h_full = [e_raw[1][:, n * H:(n + 1) * H] for n in range(2)]
        h_part = [wl_flat[:, 2 * EW + 4 * H + 2 * n * H:2 * EW + 4 * H + 2 * (n + 1) * H].rearrange(
            "p (a c s) -> p a c s", a=2, c=KH) for n in range(2)]
        xn2 = acc[0][:, 0:NT * D].rearrange("p (t d) -> p t d", d=D)
        gate = [fbuf.bitcast(fp32)[:, n * NT * NE:(n + 1) * NT * NE].rearrange("p (t e) -> p t e", e=NE) for n in range(4)]
        xn2_t = fbuf.bitcast(fp32)[:, 4 * NT * NE:4 * NT * NE + 4 * KD * P].rearrange("p (j k s) -> p j k s", j=4, k=KD)
        assert 4 * NT * NE + 4 * KD * P <= KD * NT * P // 2
        fl = f_lo[:, :, :].rearrange("p k n -> p (k n)").bitcast(fp32)
        assign = fl[:, 0:NE * NA].rearrange("p (e j) -> p e j", e=NE)
        a_scan = fl[:, NE * NA:2 * NE * NA].rearrange("p (e j) -> p e j", e=NE)
        a_pos = fl[:, 2 * NE * NA:2 * NE * NA + NA]
        a_slot = fl[:, 2 * NE * NA + NA:2 * NE * NA + 2 * NA].bitcast(i32)
        prob = [fl[:, 2 * NE * NA + (2 + n) * NA:2 * NE * NA + (2 + n) * NA + NT] for n in range(8)]
        y_in = acc[1][:, 0:8 * D].rearrange("p (j d) -> p j d", j=8)

        ps = ctx.enter_context(nc.psum_tensor("ps", [P, 8, 512], fp32))
        sort_ps = [ps[:, 4, 0:CH], ps[:, 5, 0:CH]]
        seg_ps = [ps[:, 6, :], ps[:, 7, :]]
        rank_ps = ps[:, 6, :]

        s_x = sem("x_loaded")
        s_xl = sem("x_tail_loaded")
        s_w = [sem(f"weights_loaded_{n}") for n in range(5)]
        s_lw = sem("loop_weights_loaded")
        s_edges = sem("edges_loaded")
        s_rows = sem("bias_rows_loaded")
        s_zero_st = sem("slot_rows_zeroed")
        s_const = sem("constants_ready")
        s_clear = sem("accumulator_cleared")
        s_dve = sem("dve_steps")
        s_pool = sem("pool_steps")
        s_part = sem("backward_max_half_ready")
        s_wmax = sem("weight_max_ready")
        s_wall = sem("weight_max_reduced")
        s_wsc = sem("weight_scale_ready")
        s_whi = sem("weights_hi_ready")
        s_wlo = sem("weights_lo_ready")
        s_var = sem("variance_ready")
        s_std = sem("std_ready")
        s_xn = sem("xn_ready")
        s_xt = sem("xn_transposed")
        s_fhi = sem("f_hi_ready")
        s_flo = sem("f_lo_ready")
        s_loop = sem("loop_product_ready")
        s_base = sem("loop_product_used")
        s_cnt = sem("counts_ready")
        s_tot = sem("totals_ready")
        s_inc = sem("group_chunks_ready")
        s_incp = sem("group_ends_ready")
        s_cmp = sem("chunk_compare_ready")
        s_map = sem("chunk_map_ready")
        s_mapc = sem("chunk_map_copied")
        s_proj = sem("projection_ready")
        s_phi = sem("projection_hi_staged")
        s_fix = sem("projection_lo_ready")
        s_evac = sem("projection_staged")
        s_out = [sem(f"stage_stored_{n}") for n in range(NS)]
        s_ops = sem("sort_operands_ready")
        s_used = sem("sort_operands_used")
        s_sorted = sem("sort_finished")
        s_slots = sem("slot_tables_ready")
        s_ones = sem("message_ones_ready")
        s_gath = [sem(f"gathered_{n}") for n in range(MR)]
        s_turn = sem("gather_turns")
        s_hot = sem("onehot_ready")
        s_seg = sem("chunk_summed")
        s_acc = sem("chunk_added")
        s_er = [sem(f"expert_raw_loaded_{n}") for n in range(2)]
        s_em = sem("expert_max_ready")
        s_et = sem("expert_max_transposed")
        s_ed = sem("expert_max_diagonal_ready")
        s_eb = sem("expert_max_spread")
        s_es = sem("expert_scale_ready")
        s_ehi = sem("expert_hi_ready")
        s_elo = sem("expert_lo_ready")
        s_eo = [sem(f"expert_parts_stored_{n}") for n in range(2)]
        s_x1 = sem("xn2_ready")
        s_x2t = sem("xn2_transposed")
        s_x2c = sem("xn2_t_copied")
        s_gate = sem("logits_ready")
        s_exp = sem("exp_ready")
        s_sub = sem("exp_input_ready")
        s_slot2 = sem("token_slots_ready")
        s_scat = [sem(f"rows_scattered_{n}") for n in range(4)]
        s_allscat = sem("all_rows_scattered")
        s_ew = [sem(f"expert_parts_loaded_{n}") for n in range(4)]
        s_xsin = [sem(f"slot_rows_loaded_{n}") for n in range(2)]
        s_mt = sem("slot_tile_transposed")
        s_mth = sem("slot_tile_hi_ready")
        s_mtc = sem("slot_tile_lo_ready")
        s_h = sem("hidden_ready")
        s_silu = sem("silu_ready")
        s_hf = sem("hidden_gated")
        s_hh = sem("hidden_hi_ready")
        s_hm = sem("hidden_lo_ready")
        s_y = sem("expert_result_ready")
        s_yc = sem("expert_result_copied")
        s_yo = [sem(f"expert_result_stored_{n}") for n in range(4)]
        s_yg = [sem(f"results_gathered_{n}") for n in range(4)]
        s_fin = sem("output_rows_ready")
        s_st = sem("outputs_stored")

        block = ctx.enter_context(nc.Block())

        def row(ap):
            return ap.rearrange("p a b -> p (a b)")

        def half(W, h):
            return W[h * HALF:(h + 1) * HALF].rearrange("t (p k) o -> p t (k o)", k=KD)

        def by_type(raw):
            return raw.rearrange("p (t c) -> p t c", t=HALF)

        @block.sync
        def _(sp):
            for h in range(2):
                sp.dma_start(by_type(w_raw[h]), half(Wf, h)).then_inc(s_w[h], 16)
            for b in range(NS):
                sp.sem_inc(s_out[b], 16)
            for d in range(2):
                rows = table[d].rearrange("(n b r) d -> n b (r d)", b=8, r=2)

                with sp.Fori(0, NT) as i:
                    for b in range(8):
                        sp.wait_ge(s_evac, i * 8 + (4 + d * NT * 8 + b + 1))
                        source = stage16[:, b % NS].rearrange("p t h o -> p (t h o)") if d == 0 else stage[:, b % NS, :]
                        sp.dma_start(rows[ds(i * P, P), b, :], source).then_inc(s_out[b % NS], 16)
            def load_raw(e, n):
                for m, w in enumerate((w1, w2, w3)):
                    sp.dma_start(e_raw[n][:, m * KD * H:(m + 1) * KD * H],
                                 row(w[ds(e, 1)].rearrange("e (p k) h -> (e p) k h", p=P))).then_inc(s_er[n], 16)
            with sp.Fori(0, NE // 2) as i:
                for n in range(2):
                    sp.wait_ge(s_elo, i * 2 + (n + 1))
                    load_raw(i * 2 + n, n)
            for n in range(2):
                sp.wait_ge(s_eo[n], 16 + 32 * (NE // 2))
            sp.wait_ge(s_allscat, 1)
            sp.wait_ge(s_mapc, 3)
            def load_tile(i, q):
                e = sp.value_load(expert_at[0:1, ds(i * 4 + q, 1)], min_val=0, max_val=NE - 1)
                sp.wait_ge(s_mt, i * 4 + (q + 1))
                sp.dma_start(xs_in[q % 2], xs_dram[ds((i * 4 + q) * P, P), :]).then_inc(s_xsin[q % 2], 16)
                sp.wait_ge(s_yc, i * 4 + (q + 1))
                sp.dma_start(parts[q], ew_dram[ds(e * P, P), :]).then_inc(s_ew[q], 16)

            def store_result(i, q):
                sp.dma_start(ys_dram[ds((i * 4 + q) * P, P), :], y_sb[q]).then_inc(s_yo[q], 16)
            for q in range(4):
                load_tile(0, q)
            with sp.Fori(1, NST // 4) as i:
                for q in range(4):
                    load_tile(i, q)
                    store_result(i - 1, q)
            for q in range(4):
                sp.wait_ge(s_yc, NST + q + 1)
                store_result(NST // 4 - 1, q)
            for t in range(NT):
                rows = P if t < NT - 1 else LAST
                sp.wait_ge(s_fin, t + 1)
                sp.dma_start(out[t * P:t * P + rows, :], x_sb[0:rows, t, :]).then_inc(s_st, 16)
            sp.wait_ge(s_st, 16 * NT)

        @block.scalar
        def _(act):
            act.dma_start(x_sb[:, 0:NT - 1, :], x[0:(NT - 1) * P].rearrange("(t p) d -> p t d", p=P)).then_inc(s_x, 16)
            act.wait_ge(s_const, 6)
            act.dma_start(x_sb[0:LAST, NT - 1, :], x[(NT - 1) * P:N]).then_inc(s_xl, 16)
            act.dma_start(loop_raw.rearrange("p (k o) -> p k o", k=KD), loopw.rearrange("(p k) o -> p k o", k=KD)).then_inc(s_lw, 16)
            for a, b in ((bias_f[:], fbias), (bias_b[:], bbias), (bias_s, sbias)):
                act.dma_start(a, b.partition_broadcast(P)).then_inc(s_rows, 16)
            act.dma_start(gb[:], gate_b.partition_broadcast(P)).then_inc(s_rows, 16)
            act.dma_start(gw[:], gate_w.rearrange("(p k) e -> p k e", k=KD)).then_inc(s_rows, 16)
            act.wait_ge(s_var, 1)
            nc.scalar.activation(st[:, 1], st[:, 2], ACT.Sqrt, bias=eps[:, 0:1]).then_inc(s_std, 1)
            with act.Fori(0, 5) as i:
                for j in range(5):
                    act.wait_ge(s_xt, i * 5 + (j + 1))
                    nc.scalar.copy(f_hi[:, :, ds((i * 5 + j) * P, P)],
                                   ps[:, j, 0:D].rearrange("p (k n) -> p k n", k=KD)).then_inc(s_fhi, 1)
            act.wait_ge(s_wsc, 1)
            nc.scalar.activation(loop_hi[:], loop_raw, ACT.Copy, scale=wscale[:, 2, 4:5]).then_inc(s_whi, 1)
            act.wait_ge(s_wsc, 2)
            for h in range(2):
                nc.scalar.activation(w_hi[:, 0, h * WH:(h + 1) * WH], w_raw[h], ACT.Copy,
                                     scale=wscale[:, 0, 4:5]).then_inc(s_whi, 1)
            act.wait_ge(s_wlo, 3)
            for a, b in ((e_src, src), (e_dst, dst), (e_typ, typ)):
                act.dma_start(a, b.rearrange("(p c) -> p c", c=EC)).then_inc(s_edges, 16)
            act.sem_inc(s_evac, 4)

            def low_part(i, b):
                act.wait_ge(s_fix, i * 8 + (b + 1))
                nc.scalar.copy(stage16[:, b % NS, :, 1, :],
                               ps[:, b % 4, :].rearrange("p (t o) -> p t o", t=2)).then_inc(s_evac, 1)
            with act.Fori(0, NT) as i:
                for b in range(8):
                    act.wait_ge(s_out[b % NS], i * 32 + (16 * (b // NS) + 16))
                    act.wait_ge(s_proj, i * 8 + (b + 1))
                    nc.scalar.copy(stage16[:, b % NS, :, 0, :],
                                   ps[:, b % 4, :].rearrange("p (t o) -> p t o", t=2)).then_inc(s_phi, 1)
                    if b >= 1:
                        low_part(i, b - 1)
                low_part(i, 7)
            with act.Fori(0, NT) as i:
                for b in range(8):
                    act.wait_ge(s_out[b % NS], i * 32 + (NT * 32 + 16 * (b // NS) + 16))
                    act.wait_ge(s_proj, i * 8 + (NT * 8 + b + 1))
                    nc.scalar.copy(stage[:, b % NS, :], ps[:, b % 4, :]).then_inc(s_evac, 1)
            for n in range(2):
                act.sem_inc(s_eo[n], 16)
            with act.Fori(0, NE // 2) as i:
                for n in range(2):
                    act.wait_ge(s_es, i * 2 + (n + 1))
                    act.wait_ge(s_eo[n], i * 32 + 16)
                    for m in range(3):
                        last = nc.scalar.activation(matrix(n, 0, m), e_raw[n][:, m * KD * H:(m + 1) * KD * H], ACT.Copy,
                                                    scale=emax[:, 8 + m:9 + m])
                    last.then_inc(s_ehi, 1)
                    act.wait_ge(s_ehi, i * 2 + (n + 1))
                    act.dma_start(ew_dram[ds((i * 2 + n) * P, P), 0:EW], parts[n][:, 0:EW]).then_inc(s_eo[n], 16)
                    act.wait_ge(s_elo, i * 2 + (n + 3))
                    act.dma_start(ew_dram[ds((i * 2 + n) * P, P), EW:ER], parts[n][:, EW:ER]).then_inc(s_eo[n], 16)
            act.wait_ge(s_var, 2)
            nc.scalar.activation(st[:, 1], st[:, 2], ACT.Sqrt, bias=eps[:, 0:1]).then_inc(s_std, 1)
            act.sem_inc(s_x2c, 4)
            for t in range(NT):
                act.wait_ge(s_x2t, t + 1)
                nc.scalar.copy(xn2_t[:, t % 4], ps[:, t % 4, 0:D].rearrange("p (k n) -> p k n", k=KD)).then_inc(s_x2c, 1)
            act.wait_ge(s_sub, 1)
            nc.scalar.activation(gate[2], gate[1], ACT.Exp).then_inc(s_exp, 1)

            def rows_hi(i, k):
                act.wait_ge(s_mt, i * 4 + (k + 3))
                nc.scalar.copy(xs_t[k % 2][:, 0],
                               ps[:, k % 2, 0:D].rearrange("p (k s) -> p k s", k=KD)).then_inc(s_mth, 1)

            def silu(i, k):
                act.wait_ge(s_h, i * 4 + (k + 1))
                nc.scalar.activation(h_act[k % 2], ps[:, 2 + 2 * (k % 2), :], ACT.Silu,
                                     scale=factor(k % 4, 0)).then_inc(s_silu, 1)

            def hidden_hi(i, k):
                act.wait_ge(s_hf, i * 4 + (k + 1))
                nc.scalar.copy(h_part[k % 2][:, 0].rearrange("p c s -> p (c s)"), h_full[k % 2]).then_inc(s_hh, 1)

            def result(i, k):
                act.wait_ge(s_yo[k], i * 16 + 16)
                act.wait_ge(s_y, i * 4 + (k + 1))
                nc.scalar.activation(y_sb[k], ps[:, 6 + k % 2, 0:D], ACT.Copy,
                                     scale=factor(k % 4, 2)).then_inc(s_yc, 1)

            def expert_steps(i, last):
                for k in range(4):
                    if not last or k < 3:
                        silu(i, k + 1)
                    if not last or k < 2:
                        rows_hi(i, k + 2)
                    if not last or k < 3:
                        hidden_hi(i, k + 1)
                    result(i, k)
            act.sem_inc(s_yc, 4)
            for n in range(4):
                act.sem_inc(s_yo[n], 16)
            rows_hi(0, 0)
            silu(0, 0)
            rows_hi(0, 1)
            hidden_hi(0, 0)
            with act.Fori(0, NST // 4 - 1) as i:
                expert_steps(i, False)
            expert_steps(NST // 4 - 1, True)

        @block.gpsimd
        def _(pool):
            chain = Chain(pool, s_pool)
            nc.gpsimd.iota(iota_p[:], [[1, P]], base=0, channel_multiplier=0,
                           allow_small_or_imprecise_dtypes=True).then_inc(s_const, 1)
            nc.gpsimd.iota(iota_ch[:], [[1, CH]], base=0, channel_multiplier=0,
                           allow_small_or_imprecise_dtypes=True).then_inc(s_const, 1)
            nc.gpsimd.iota(iota_row[:], [[0, 1]], base=0, channel_multiplier=1,
                           allow_small_or_imprecise_dtypes=True).then_inc(s_const, 1)
            nc.gpsimd.memset(ones[:], 1.0).then_inc(s_const, 1)
            nc.gpsimd.memset(eps[:], EPS).then_inc(s_const, 1)
            nc.gpsimd.memset(x_sb[:, NT - 1, :], 0.0).then_inc(s_const, 1)
            nc.gpsimd.memset(zeros16[:], 0.0)
            nc.gpsimd.memset(msg[:, :, 0:1], 1.0)
            nc.gpsimd.memset(msg16[:, :, 2 + 2 * D:4 + 2 * D], 1.0).then_inc(s_ones, 1)
            for n, block_ in enumerate((2, 0)):
                pool.wait_ge(s_wmax, n + 1)
                nc.gpsimd.partition_all_reduce(wscale[:, block_, 2:3], wscale[:, block_, 0:1], P,
                                               bass.bass_isa.ReduceOp.max).then_inc(s_wall, 1)
            pool.wait_ge(s_wlo, 3)
            pool.dma_start(by_type(w_raw[0]), half(Wb, 0)).then_inc(s_w[2], 16)
            pool.wait_ge(s_part, 1)
            pool.dma_start(by_type(w_raw[0]), half(Wb, 1)).then_inc(s_w[3], 16)
            pool.wait_ge(s_wmax, 3)
            nc.gpsimd.partition_all_reduce(wscale[:, 1, 2:3], wscale[:, 1, 0:1], P,
                                           bass.bass_isa.ReduceOp.max).then_inc(s_wall, 1)
            pool.wait_ge(s_wlo, 4)
            pool.dma_start(by_type(w_raw[0]), half(Wb, 0)).then_inc(s_w[4], 16)
            pool.wait_ge(s_clear, 1)
            for n in range(4):
                pool.dma_start(xs_dram.rearrange("(p a) d -> p (a d)", p=P)[:, n * 4096:(n + 1) * 4096],
                               acc[0][:, 0:4096]).then_inc(s_zero_st, 16)
            for d in range(2):
                pool.wait_ge(s_slots, d + 1)
                for b in range(NS):
                    pool.wait_ge(s_out[b], 16 + 32 * NT * (d + 1))
                with pool.Fori(0, CH // 16) as i:
                    chain.n = i * 2 + (2 * (CH // 16) * d)
                    for j in range(16):
                        if j % 8 == 0:
                            chain.link(nc.gpsimd.tensor_copy(idx_now[:, j // 8, :], slot_row[d][:, ds(i * 16 + j, 8)]))
                        pool.wait_ge(s_seg, i * 16 + (d * CH + j + SR - MR + 1))
                        pool.sem_inc(s_turn, 1)
                        to = msg16[:, j % MR, 2:2 + 2 * D] if d == 0 else msg[:, j % MR, 1:1 + D]
                        pool.indirect_dma_start(to, None, table[d],
                                                bass.IndirectOffsetOnAxis(idx_now[:, j // 8, j % 8:j % 8 + 1], 0)
                                                ).then_inc(s_gath[j % MR], 16)
            pool.wait_ge(s_slot2, 1)
            pool.wait_ge(s_zero_st, 64)
            for n in range(NA):
                t = n % NT
                rows = P if t < NT - 1 else LAST
                if n >= 4:
                    pool.wait_ge(s_scat[n % 4], 16 * (n // 4))
                pool.indirect_dma_start(xs_dram, bass.IndirectOffsetOnAxis(a_slot[0:rows, n:n + 1], 0),
                                        xn2[0:rows, t, :], None).then_inc(s_scat[n % 4], 16)
            for n in range(4):
                pool.wait_ge(s_scat[n], 16 * len(range(n, NA, 4)))
            pool.sem_inc(s_allscat, 1)
            for q in range(4):
                pool.wait_ge(s_yo[q], 16 + 16 * (NST // 4))
            for t in range(NT):
                rows = P if t < NT - 1 else LAST
                if t >= 4:
                    pool.wait_ge(s_fin, t - 3)
                for c in range(2):
                    pool.indirect_dma_start(y_in[0:rows, 2 * (t % 4) + c, :], None, ys_dram,
                                            bass.IndirectOffsetOnAxis(a_slot[0:rows, c * NT + t:c * NT + t + 1], 0)
                                            ).then_inc(s_yg[t % 4], 16)

        @block.tensor
        def _(pe):
            mm = nc.tensor.matmul

            def sort_chunk(n, d, j):
                j = j % OR[d]
                pe.wait_ge(s_ops, n + 1)
                mm(sort_ps[0], ops_a[j][:, 0, :], ops_b[j], start=False, stop=False,
                   skip_group_check=True)
                mm(sort_ps[1], ops_a[j][:, 1, :], ops_b[j], start=False, stop=False,
                   skip_group_check=True).then_inc(s_used, 1)

            def sort_open():
                for q in range(2):
                    mm(sort_ps[q], zeros16[0:1, :], iota_ch[0:1, :], start=True, stop=False, skip_group_check=True)

            def sort_close():
                for q in range(2):
                    last = mm(sort_ps[q], zeros16[0:1, :], iota_ch[0:1, :], start=False, stop=True,
                              skip_group_check=True)
                last.then_inc(s_sorted, 1)

            def segment_chunk(d, n, base, j):
                pe.wait_ge(s_hot, n + 1)
                pe.wait_ge(s_gath[j % MR], base * 32 + 16 * (j // MR + 1))
                pe.wait_ge(s_acc, n + 1)
                to = seg_ps[j % 2]
                if d == 0:
                    m = msg16[:, j % MR, :]
                    mm(to[:, 0:D + 1], onehot16[:, j % SR, 0:P], m[:, 2 + D:3 + 2 * D], start=True, stop=False)
                    mm(to[:, 0:D], onehot16[:, j % SR, 0:P], m[:, 2:2 + D], start=False, stop=True).then_inc(s_seg, 1)
                else:
                    mm(to[:, 0:D + 1], onehot[:, j % SR, :], msg[:, j % MR, 0:D + 1], start=True,
                       stop=True).then_inc(s_seg, 1)

            def three(to, pairs, sem_):
                for n, (stationary, moving) in enumerate(pairs):
                    last = mm(to, stationary, moving, start=(n == 0), stop=(n == len(pairs) - 1),
                              skip_group_check=True)
                if sem_ is not None:
                    last.then_inc(sem_, 1)

            def project(i, d, b):
                h, q = b // 4, b % 4
                pe.wait_ge(s_evac, i * 8 + (d * NT * 8 + b + 1))

                def w(part, k):
                    return part[:, d, h * WH:(h + 1) * WH].rearrange("p (t k o) -> p t k o", k=KD, o=D)[
                        :, 2 * q:2 * q + 2, k, :]
                three(ps[:, q, :], [(f[:, k, ds(i * P, P)], w(part, k)) for k in range(KD)
                                    for f, part in ((f_hi, w_hi), (f_hi, w_lo), (f_lo, w_hi))], s_proj)

            def subtract_high(i, b):
                pe.wait_ge(s_phi, i * 8 + (b + 1))
                mm(ps[:, b % 4, :].rearrange("p (t o) -> p t o", t=2), minus16[:], stage16[:, b % NS, :, 0, :],
                   start=False, stop=True, skip_group_check=True).then_inc(s_fix, 1)

            def forward_tile(i, sort):
                for b in range(8):
                    project(i, 0, b)
                    if sort is not None:
                        for j in range(b * A_SORT // 8, (b + 1) * A_SORT // 8):
                            sort_chunk(sort * A_SORT + j, 0, j)
                    if b >= 1:
                        subtract_high(i, b - 1)
                subtract_high(i, 7)

            pe.wait_ge(s_const, 10)
            pe.wait_ge(s_ones, 1)
            pe.sem_inc(s_flo, 5)
            with pe.Fori(0, 5) as i:
                for j in range(5):
                    pe.wait_ge(s_xn, i * 5 + (j + 1))
                    pe.wait_ge(s_flo, i * 5 + (j + 1))
                    for k in range(KD):
                        last = nc.tensor.transpose(ps[:, j, k * P:(k + 1) * P], xn[:, j, k::KD], ident[:])
                    last.then_inc(s_xt, 1)
            pe.wait_ge(s_flo, NT + 5)
            pe.wait_ge(s_wlo, 3)
            with pe.Fori(0, PRE0) as i:
                forward_tile(i, None)

            def rank_products(cnt, rows, groups, chunks, n):
                pe.wait_ge(s_cnt, n + 1)
                mm(rank_ps[:, 0:groups], before[0:rows, :], cnt, start=True, stop=True)
                mm(rank_ps[:, 32:32 + groups], ones16[0:rows, :], cnt, start=True, stop=True)
                mm(rank_ps[0:groups, 64:65], cnt, ones16[0:rows, 0:1], start=True, stop=True).then_inc(s_tot, 1)
                pe.wait_ge(s_inc, n + 1)
                mm(rank_ps[0:groups, 65:66], upto[0:groups, 0:groups], small[0:groups, 8, 0:1],
                   start=True, stop=True).then_inc(s_incp, 1)
                pe.wait_ge(s_cmp, n + 1)
                mm(ps[0:1, 7, 0:chunks], ones[0:groups, 0:1], onehot_flat[0:groups, 0:chunks],
                   start=True, stop=True).then_inc(s_map, 1)

            for d in range(2):
                rank_products(cnt16[0:EP, 0:NT], EP, NT, CH, d)
            pe.sem_inc(s_base, 2)

            def self_product(t, j):
                pe.wait_ge(s_base, t + 1)
                three(ps[:, 4 + j, 0:D], [(f[:, k, ds(t * P, P)], w[:, k * D:(k + 1) * D]) for k in range(KD)
                                          for f, w in ((f_hi, loop_hi), (f_hi, loop_lo), (f_lo, loop_hi))], s_loop)
            with pe.Fori(0, NT // 2) as i:
                for j in range(2):
                    self_product(i * 2 + j, j)
            self_product(NT - 1, 0)
            with pe.Fori(PRE0, PRE) as i:
                forward_tile(i, None)
            pe.wait_ge(s_base, NT + 2)
            pe.sem_inc(s_used, OR[0])
            sort_open()
            with pe.Fori(0, NT - PRE) as i:
                forward_tile(i + PRE, i)
            sort_close()
            pe.wait_ge(s_wlo, 5)
            pe.wait_ge(s_slots, 1)
            sort_open()
            pe.sem_inc(s_seg, SR)
            with pe.Fori(0, NT) as i:
                for b in range(8):
                    project(i, 1, b)
                    for j in range(b * B_SORT // 8, (b + 1) * B_SORT // 8):
                        sort_chunk(i * B_SORT + (EC + j), 1, j)
                    for j in range(2 * b, 2 * b + 2):
                        segment_chunk(0, i * 16 + j, i, j)
            sort_close()
            for j in range(16):
                segment_chunk(0, NT * 16 + j, NT, j)
            pe.sem_inc(s_elo, 2)
            with pe.Fori(0, NE) as i:
                for j in range(16):
                    segment_chunk(1, i * 16 + (CH + j), i + CH // 16, j)
                    if j == 3:
                        pe.wait_ge(s_em, i + 1)
                        nc.tensor.transpose(ps[0:3, 0, 0:P], emax[:, 0:3], ident[:]).then_inc(s_et, 1)
                    if j == 9:
                        pe.wait_ge(s_ed, i + 1)
                        mm(ps[:, 1, 0:3], ones[0:3, :], emax[0:3, 4:7], start=True, stop=True).then_inc(s_eb, 1)
            with pe.Fori(NE, CH // 16) as i:
                for j in range(16):
                    segment_chunk(1, i * 16 + (CH + j), i + CH // 16, j)
            for t in range(NT + 1):
                if t < NT:
                    pe.wait_ge(s_x1, t + 1)
                    pe.wait_ge(s_x2c, t + 1)
                    for k in range(KD):
                        last = nc.tensor.transpose(ps[:, t % 4, k * P:(k + 1) * P], xn2[:, t, k::KD], ident[:])
                    last.then_inc(s_x2t, 1)
                if t >= 1:
                    pe.wait_ge(s_x2c, t + 4)
                    for k in range(KD):
                        last = mm(ps[:, 4, (t - 1) * NE:t * NE], xn2_t[:, (t - 1) % 4, k, :], gw[:, k, :],
                                  start=(k == 0), stop=(k == KD - 1))
            last.then_inc(s_gate, 1)
            rank_products(cnt16[:, 0:NE], P, NE, NST, 2)
            pe.wait_ge(s_mapc, 3)

            def transpose_rows(i, k):
                pe.wait_ge(s_xsin[k % 2], i * 32 + 16 * (k // 2 + 1))
                for j in range(KD):
                    last = nc.tensor.transpose(ps[:, k % 2, j * P:(j + 1) * P], xs_in[k % 2][:, j::KD], ident[:])
                last.then_inc(s_mt, 1)

            def hidden(i, k):
                pe.wait_ge(s_mtc, i * 4 + (k + 1))
                pe.wait_ge(s_ew[k % 4], i * 16 + 16 * (k // 4 + 1))
                for m in range(2):
                    w = [matrix(k % 4, low, m).rearrange("p (k h) -> p k h", k=KD) for low in range(2)]
                    for c in range(KH):
                        pairs = [(w[a][:, j, c::KH], xs_t[k % 2][:, b, j, :]) for j in range(KD)
                                 for a, b in ((0, 0), (0, 1), (1, 0))]
                        three(ps[:, 2 + 2 * (k % 2) + m, c * P:(c + 1) * P], pairs,
                              s_h if (m, c) == (1, KH - 1) else None)

            def result(i, k):
                pe.wait_ge(s_hm, i * 4 + (k + 1))
                pe.wait_ge(s_yc, i * 4 + (k + 3))
                w = [matrix(k % 4, low, 2).rearrange("p (c o) -> p c o", c=KH) for low in range(2)]
                pairs = [(h_part[k % 2][:, b, c, :], w[a][:, c, :]) for c in range(KH) for a, b in ((0, 0), (1, 0), (0, 1))]
                three(ps[:, 6 + k % 2, 0:D], pairs, s_y)

            def expert_steps(i, last):
                for k in range(4):
                    if not last or k < 3:
                        hidden(i, k + 1)
                    if not last or k < 2:
                        transpose_rows(i, k + 2)
                    result(i, k)
            pe.sem_inc(s_mt, 2)
            transpose_rows(0, 0)
            hidden(0, 0)
            transpose_rows(0, 1)
            with pe.Fori(0, NST // 4 - 1) as i:
                expert_steps(i, False)
            expert_steps(NST // 4 - 1, True)

        @block.vector
        def _(dve):
            v = nc.vector
            chain = Chain(dve, s_dve)
            mark, link = chain.mark, chain.link

            def fence():
                link(v.memset(fence_cell[:], 0.0))

            def layernorm_stats(nth):
                me, mo = stats[:, :, 1], stats[:, :, 4]
                fence()
                mark(v.tensor_tensor(st[:, 4], me, mo, ALU.subtract))
                mark(v.tensor_tensor(st[:, 3], me, mo, ALU.add))
                link(v.tensor_tensor(st[:, 2], stats[:, :, 2], stats[:, :, 5], ALU.add))
                link(v.scalar_tensor_tensor(st[:, 5], st[:, 4], 0.25, st[:, 4], ALU.mult, ALU.mult))
                v.scalar_tensor_tensor(st[:, 2], st[:, 2], 1.0 / D, st[:, 5], ALU.mult, ALU.add).then_inc(s_var, 1)
                mark(v.tensor_scalar(mean, st[:, 3], 0.5, None, ALU.mult))
                dve.wait_ge(s_std, nth)
                link(v.reciprocal(rstd, st[:, 1]))

            def largest(out_, raw):
                return v.tensor_reduce(out_, raw, AX.X, ALU.max, apply_absolute_value=True)

            def power_of_two(big, up, down):
                link(v.tensor_scalar(big, big, 1e-30, None, ALU.max))
                link(v.tensor_scalar(up.bitcast(i32), big.bitcast(i32), EXP_MASK, None, ALU.bitwise_and))
                return v.tensor_scalar(down.bitcast(i32), up.bitcast(i32), -1.0, EXP_TWICE_BIAS, ALU.mult, ALU.add)

            def weight_scale(block_, nth):
                dve.wait_ge(s_wall, nth)
                w = wscale[:, block_]
                power_of_two(w[:, 2:3], w[:, 3:4], w[:, 4:5]).then_inc(s_wsc, 1)
                dve.wait_ge(s_wsc, nth)
                link(v.tensor_scalar(w[:, 5:6], w[:, 3:4], 2.0, None, ALU.mult))

            def weight_low(lo, hi, raw, block_, nth):
                dve.wait_ge(s_whi, nth)
                v.scalar_tensor_tensor(lo, raw, wscale[:, block_, 4:5], hi, ALU.mult, ALU.subtract).then_inc(s_wlo, 1)

            dve.wait_ge(s_const, 6)
            v.tensor_scalar(ident[:], iota_p[:], iota_row[:], None, ALU.is_equal)
            v.tensor_scalar(before[:], iota_p[:], iota_row[:], None, ALU.is_gt).then_inc(s_const, 1)
            v.tensor_scalar(upto[:], iota_p[:, 0:32], iota_row[:], None, ALU.is_ge)
            v.tensor_scalar(minus16[:], iota_p[:], iota_row[:], -1.0, ALU.is_equal, ALU.mult)
            v.tensor_copy(ones16[:], ones[:])
            v.tensor_copy(iota_p16[:], iota_p[:])
            link(v.memset(valid[:], 1.0))
            mark(v.tensor_scalar(valid[:, NT - 1:NT], iota_row[:], float(LAST), None, ALU.is_lt))
            v.memset(small[:], 0.0).then_inc(s_const, 3)
            dve.wait_ge(s_x, 16)
            dve.wait_ge(s_xl, 16)
            with dve.Fori(0, NT) as t:
                v.bn_stats(row(stats[:, ds(t, 1), :]), row(x_sb[:, ds(t, 1), :]))
            layernorm_stats(1)
            dve.wait_ge(s_lw, 16)
            largest(wscale[:, 2, 0:1], loop_raw).then_inc(s_wmax, 1)
            for h in range(2):
                dve.wait_ge(s_w[h], 16)
                link(largest(wscale[:, 0, h:h + 1], w_raw[h]))
            v.tensor_tensor(wscale[:, 0, 0:1], wscale[:, 0, 0:1], wscale[:, 0, 1:2], ALU.max).then_inc(s_wmax, 1)
            with dve.Fori(0, 5) as i:
                for j in range(5):
                    t = i * 5 + j
                    v.tensor_scalar(xn[:, j, :], row(x_sb[:, ds(t, 1), :]), st[:, 0, ds(t, 1)], st[:, 1, ds(t, 1)],
                                    ALU.subtract, ALU.mult).then_inc(s_xn, 1)
                for j in range(5):
                    t = i * 5 + j
                    dve.wait_ge(s_fhi, t + 1)
                    v.tensor_tensor(f_lo[:, :, ds(t * P, P)], ps[:, j, 0:D].rearrange("p (k n) -> p k n", k=KD),
                                    f_hi[:, :, ds(t * P, P)], ALU.subtract).then_inc(s_flo, 1)
            weight_scale(2, 1)
            weight_scale(0, 2)
            weight_low(loop_lo[:], loop_hi[:], loop_raw, 2, 1)
            for h in range(2):
                weight_low(w_lo[:, 0, h * WH:(h + 1) * WH], w_hi[:, 0, h * WH:(h + 1) * WH], w_raw[h], 0, h + 2)

            def group_ends(groups, n, first):
                g = slice(0, groups)
                dve.wait_ge(s_tot, n + 1)
                mark(v.tensor_copy(small[:, 1, g], rank_ps[:, 0:groups]))
                mark(v.tensor_scalar(small_i[:, 0, g], rank_ps[:, 32:32 + groups], float(P - 1), None, ALU.add))
                link(v.tensor_scalar(small_i[0:groups, 1, 0:1], rank_ps[0:groups, 64:65], float(P - 1), None, ALU.add))
                mark(v.tensor_scalar(small_i[:, 0, g], small_i[:, 0, g], 7, None, ALU.arith_shift_right))
                link(v.tensor_scalar(small_i[0:groups, 1, 0:1], small_i[0:groups, 1, 0:1], 7, None,
                                     ALU.arith_shift_right))
                mark(v.tensor_copy(small[:, 2, g], small_i[:, 0, g]))
                v.tensor_copy(small[0:groups, 8, 0:1], small_i[0:groups, 1, 0:1]).then_inc(s_inc, 1)
                dve.wait_ge(s_inc, n + 1)
                link(v.tensor_tensor_scan(small[:, 3, g], small[:, 2, g], small[:, 2, g], 0.0, ALU.add, ALU.max))
                link(v.tensor_tensor(small[:, 4, g], small[:, 3, g], small[:, 2, g], ALU.subtract))
                link(v.scalar_tensor_tensor(first, small[:, 4, g], float(P), small[:, 1, g], ALU.mult, ALU.add))

            def chunk_map(groups, chunks, n, out_i, scale, last_group):
                dve.wait_ge(s_incp, n + 1)
                link(v.tensor_copy(small[0:groups, 9, 0:1], rank_ps[0:groups, 65:66]))
                v.tensor_scalar(onehot_flat[0:groups, 0:chunks], iota_ch[0:groups, 0:chunks],
                                small[0:groups, 9, 0:1], None, ALU.is_ge).then_inc(s_cmp, 1)
                dve.wait_ge(s_map, n + 1)
                v.tensor_scalar(out_i, ps[0:1, 7, 0:chunks], float(last_group), float(scale),
                                ALU.min, ALU.mult).then_inc(s_mapc, 1)

            dve.wait_ge(s_edges, 48)
            first_slot = [small[:, 5, 0:NT], small[:, 10, 0:NT]]
            for d, (target, source) in enumerate(((e_dst, e_src), (e_src, e_dst))):
                link(v.tensor_scalar(e_int, target, 7, None, ALU.arith_shift_right))
                mark(v.tensor_copy(e_key[:, d, :], e_int))
                mark(v.tensor_scalar(pay_2[d], source, -SRC_BIAS, None, ALU.add))
                link(v.scalar_tensor_tensor(e_scan, e_int, -float(P), target, ALU.mult, ALU.add))
                link(v.scalar_tensor_tensor(e_pos, e_typ, float(P), e_scan, ALU.mult, ALU.add))
                mark(v.tensor_scalar(pay_1[d], e_pos, 1.0, None, ALU.add))
                n0 = chain.n
                with dve.Fori(0, NT) as g:
                    chain.n = g + n0
                    link(v.tensor_scalar(e_eq[:, 0, :], e_key[:, d, :], iota_p[0:EP, ds(g, 1)], None, ALU.is_equal,
                                         ALU.add, accum_out=small[0:EP, 0, ds(g, 1)]))
                chain.n = n0 + NT
                link(v.tensor_copy(cnt16[0:EP, 0:NT], small[0:EP, 0, 0:NT]))
                dve.sem_inc(s_cnt, 1)
                group_ends(NT, d, first_slot[d])
                chunk_map(NT, CH, d, tile_at[d][:], AW, NT - 1)
            dve.wait_ge(s_w[2], 16)
            largest(wscale[:, 1, 0:1], w_raw[0]).then_inc(s_part, 1)
            dve.wait_ge(s_rows, 80)
            n0 = chain.n

            def self_loop(t, j, n):
                xt = row(x_sb[:, ds(t, 1), :])
                dve.wait_ge(s_loop, t + 1)
                chain.n = n
                link(v.scalar_tensor_tensor(xt, ps[:, 4 + j, 0:D], wscale[:, 2, 5:6], xt, ALU.mult, ALU.add))
                v.tensor_tensor(xt, xt, bias_s, ALU.add).then_inc(s_base, 1)
            with dve.Fori(0, NT // 2) as i:
                for j in range(2):
                    self_loop(i * 2 + j, j, i * 2 + (n0 + j))
            self_loop(NT - 1, 0, n0 + NT - 1)
            chain.n = n0 + NT
            dve.wait_ge(s_w[3], 16)
            dve.wait_ge(s_part, 1)
            link(largest(wscale[:, 1, 1:2], w_raw[0]))
            v.tensor_tensor(wscale[:, 1, 0:1], wscale[:, 1, 0:1], wscale[:, 1, 1:2], ALU.max).then_inc(s_wmax, 1)

            def slots_of_edges(d):
                def equal(buf, g):
                    return v.tensor_scalar(e_eq[:, buf, :], e_key[:, d, :], iota_p[0:EP, ds(g, 1)], None, ALU.is_equal)

                def count(buf, g):
                    return v.tensor_tensor_scan(e_scan, e_eq[:, buf, :], e_eq[:, buf, :],
                                                first_slot[d][0:EP, ds(g, 1)], ALU.add, ALU.max)

                def take(buf):
                    return v.copy_predicated(e_pos, e_eq[:, buf, :].bitcast(u16), e_scan)
                link(equal(0, 0))
                link(count(0, 0))
                n1 = chain.n
                with dve.Fori(0, NT // 2) as g2:
                    chain.n = g2 * 6 + n1
                    for q in range(2):
                        mark(equal(1 - q, g2 * 2 + (q + 1)))
                        mark(take(q))
                        dve.wait_ge(s_dve, chain.n)
                        link(count(1 - q, g2 * 2 + (q + 1)))
                chain.n = n1 + (NT // 2) * 6
                link(take(0))
                link(v.tensor_scalar(e_int, e_pos, -1.0, None, ALU.add))
                link(v.tensor_copy(e_scan, e_int))
                link(v.tensor_scalar(e_int, e_int, 7, None, ALU.arith_shift_right))
                link(v.tensor_copy(pos_b[d], e_int))
                link(v.scalar_tensor_tensor(pos_a[d], pos_b[d], -float(P), e_scan, ALU.mult, ALU.add))

            def backward_half(h, nth_load, nth):
                dve.wait_ge(s_w[nth_load], 16)
                hi = w_hi[:, 1, h * WH:(h + 1) * WH]
                v.tensor_scalar(hi, w_raw[0], wscale[:, 1, 4:5], None, ALU.mult).then_inc(s_whi, 1)
                weight_low(w_lo[:, 1, h * WH:(h + 1) * WH], hi, w_raw[0], 1, nth)

            slots_of_edges(0)
            weight_scale(1, 3)
            backward_half(1, 3, 4)
            slots_of_edges(1)
            backward_half(0, 4, 5)
            dve.wait_ge(s_wlo, 5)
            v.memset(acc[0][:], 0.0).then_inc(s_clear, 1)

            def sort_operands(d, n, col, j):
                j = j % OR[d]
                dve.wait_ge(s_used, n + (1 + OR[0] - OR[d]))
                v.tensor_scalar(ops_b[j], iota_ch[0:EP, :], pos_b[d][:, ds(col, 1)], None, ALU.is_equal)
                v.tensor_scalar(ops_a[j][:, 0, :], iota_p16[0:EP, :], pos_a[d][:, ds(col, 1)],
                                pay_1[d][:, ds(col, 1)], ALU.is_equal, ALU.mult)
                v.tensor_scalar(ops_a[j][:, 1, :], iota_p16[0:EP, :], pos_a[d][:, ds(col, 1)],
                                pay_2[d][:, ds(col, 1)], ALU.is_equal, ALU.mult).then_inc(s_ops, 1)

            def slot_tables(d):
                tmp, tmp_i = onehot_flat[:, 0:CH], onehot_flat[:, CH:2 * CH].bitcast(i32)
                dve.wait_ge(s_sorted, d + 1)
                mark(v.tensor_scalar(tmp, sort_ps[0], -1.0, None, ALU.add))
                link(v.tensor_scalar(tmp_i, sort_ps[0], -1.0, 0.0, ALU.add, ALU.max))
                link(v.tensor_scalar(tmp_i, tmp_i, 7, None, ALU.arith_shift_right))
                link(v.scalar_tensor_tensor(slot_loc[d][:], tmp_i, -float(P), tmp, ALU.mult, ALU.add))
                link(v.tensor_scalar(tmp, sort_ps[1], SRC_BIAS, float(R), ALU.add, ALU.mult))
                link(v.tensor_tensor(slot_row[d][:], tmp, tmp_i, ALU.add))
                dve.sem_inc(s_slots, 1)

            tile_regs = [dve.alloc_register(f"tile_reg_{q}") for q in range(4)]

            def onehot_chunk(d, n, col, j):
                dve.wait_ge(s_seg, n + 1)
                to, iota = (onehot16[:, j % SR, 0:P], iota_p16) if d == 0 else (onehot[:, j % SR, :], iota_p)
                v.tensor_scalar(to, iota[:], slot_loc[d][:, ds(col, 1)], None, ALU.is_equal).then_inc(s_hot, 1)

            def load_tiles(d, col):
                dve.load(tile_regs, tile_at[d][0:1, ds(col, 4)])
                return [dve.snap(r, min_val=0, max_val=(NT - 1) * AW) for r in tile_regs]

            def add_chunk(d, n, j, at):
                dve.wait_ge(s_seg, n + (SR + 1))
                dve.wait_ge(s_acc, n + 2)
                a = acc[d][:, ds(at, D + 1)]
                v.tensor_tensor(a, a, seg_ps[j % 2][:, 0:D + 1], ALU.add).then_inc(s_acc, 1)

            def sums_turn(d, i, more=True, sort=None, steps=None):
                for j0 in range(0, 16, 2):
                    for j in (j0 + 2, j0 + 3):
                        if sort == "on" or sort == "last" and j < B_SORT:
                            sort_operands(1, i * B_SORT + (EC + j), i * B_SORT + j, j)
                    for j in (j0, j0 + 1):
                        if more or j < 16 - LEAD:
                            onehot_chunk(d, i * 16 + (d * CH + j + LEAD), i * 16 + (j + LEAD), j + LEAD)
                    if j0 % 4 == 0:
                        at = load_tiles(d, i * 16 + j0)
                    for j in (j0, j0 + 1):
                        add_chunk(d, i * 16 + (d * CH + j), j, at[j % 4])
                    if steps is not None and j0 in steps:
                        steps[j0]()

            with dve.Fori(0, EC // OR[0]) as i:
                for j in range(OR[0]):
                    sort_operands(0, i * OR[0] + j, i * OR[0] + j, j)
            slot_tables(0)
            dve.wait_ge(s_zero_st, 64)
            dve.sem_inc(s_acc, 2)
            for j in range(LEAD):
                onehot_chunk(0, j, j, j)
            for j in range(2):
                sort_operands(1, EC + j, j, j)
            with dve.Fori(0, NT - 1) as i:
                sums_turn(0, i, sort="on")
            sums_turn(0, NT - 1, sort="last")
            sums_turn(0, NT, more=False)
            dve.wait_ge(s_seg, CH + SR)
            slot_tables(1)
            link(v.memset(acc[1][:], 0.0))
            for j in range(LEAD):
                onehot_chunk(1, CH + j, j, j)

            def degrees(d):
                deg = acc[d][:, :].rearrange("p (t a) -> p t a", a=AW)[:, :, DEG[d]]
                mark(v.tensor_scalar(small[:, 2 * d + 1, 0:NT], deg, 1.0, None, ALU.min))
                link(v.tensor_scalar(small[:, 2 * d, 0:NT], deg, 1.0, None, ALU.max))
                link(v.reciprocal(small[:, 2 * d, 0:NT], small[:, 2 * d, 0:NT]))
                link(v.tensor_scalar(small[:, 2 * d, 0:NT], small[:, 2 * d, 0:NT], wscale[:, d, 3:4], None, ALU.mult))

            def add_mean(d, t):
                xt = row(x_sb[:, ds(t, 1), :])
                bias = (bias_f, bias_b)[d]
                link(v.scalar_tensor_tensor(xt, acc[d][:, ds(t * AW + SUM0[d], D)], small[:, 2 * d, ds(t, 1)], xt,
                                            ALU.mult, ALU.add))
                link(v.scalar_tensor_tensor(xt, bias[:], small[:, 2 * d + 1, ds(t, 1)], xt, ALU.mult, ALU.add))

            dve.wait_ge(s_acc, CH + 2)
            degrees(0)

            n0 = chain.n
            TURN = 10

            def expert_turn(i, e, n):
                def maxima():
                    dve.wait_ge(s_er[n], i * 48 + 48)
                    for m in range(3):
                        last = largest(emax[:, m:m + 1], e_raw[n][:, m * KD * H:(m + 1) * KD * H])
                    last.then_inc(s_em, 1)

                def diagonal():
                    dve.wait_ge(s_et, e + 1)
                    link(v.tensor_reduce(emax[0:3, 3:4], ps[0:3, 0, 0:P], AX.X, ALU.max))
                    v.tensor_scalar(emax[0:3, 4:7], ident[0:3, 0:3], emax[0:3, 3:4], None, ALU.mult).then_inc(s_ed, 1)

                def scales():
                    dve.wait_ge(s_eb, e + 1)
                    dve.wait_ge(s_eo[n], i * 32 + 16)
                    link(v.tensor_scalar(escale[:, 0:3], ps[:, 1, 0:3], 1e-30, None, ALU.max))
                    link(v.tensor_scalar(escale[:, 3:6].bitcast(i32), escale[:, 0:3].bitcast(i32), EXP_MASK, None,
                                         ALU.bitwise_and))
                    link(v.tensor_scalar(emax[:, 8:11].bitcast(i32), escale[:, 3:6].bitcast(i32), -1.0,
                                         EXP_TWICE_BIAS, ALU.mult, ALU.add))
                    mark(v.tensor_copy(factor(n, 0), escale[:, 3:4]))
                    mark(v.tensor_scalar(factor(n, 1), emax[:, 8:9], 0.125, None, ALU.mult))
                    link(v.tensor_scalar(escale[:, 6:7], escale[:, 3:4], escale[:, 4:5], escale[:, 5:6],
                                         ALU.mult, ALU.mult))
                    link(v.tensor_scalar(factor(n, 2), escale[:, 6:7], 8.0, None, ALU.mult))
                    dve.sem_inc(s_es, 1)

                def low_parts():
                    dve.wait_ge(s_ehi, e + 1)
                    for m in range(3):
                        last = v.scalar_tensor_tensor(matrix(n, 1, m), e_raw[n][:, m * KD * H:(m + 1) * KD * H],
                                                      emax[:, 8 + m:9 + m], matrix(n, 0, m), ALU.mult, ALU.subtract)
                    last.then_inc(s_elo, 1)

                def mean_of_tile():
                    add_mean(0, e)
                chain.n = i * (2 * TURN) + (n0 + TURN * n)
                sums_turn(1, e, steps={0: maxima, 4: diagonal, 6: mean_of_tile, 10: scales, 14: low_parts})
            with dve.Fori(0, NE // 2) as i:
                for n in range(2):
                    expert_turn(i, i * 2 + n, n)
            chain.n = n0 + NE * TURN
            n0 = chain.n
            with dve.Fori(NE, CH // 16 - 1) as i:
                chain.n = (i - NE) * 2 + n0
                sums_turn(1, i, steps={6: lambda: add_mean(0, i)})
            chain.n = n0 + 2 * (CH // 16 - 1 - NE)
            sums_turn(1, CH // 16 - 1, more=False)
            dve.wait_ge(s_acc, 2 * CH + 2)
            degrees(1)
            n0 = chain.n
            with dve.Fori(0, NT) as t:
                chain.n = t * 2 + n0
                add_mean(1, t)
                v.bn_stats(row(stats[:, ds(t, 1), :]), row(x_sb[:, ds(t, 1), :]))
            chain.n = n0 + 2 * NT
            mark(v.memset(small[:, 7, :], 0.0))
            layernorm_stats(2)
            with dve.Fori(0, NT) as t:
                v.tensor_scalar(row(xn2[:, ds(t, 1), :]), row(x_sb[:, ds(t, 1), :]), st[:, 0, ds(t, 1)],
                                st[:, 1, ds(t, 1)], ALU.subtract, ALU.mult).then_inc(s_x1, 1)

            def over_e(a):
                return a.unsqueeze(2).to_broadcast([P, NT, NE])
            link(v.tensor_scalar(small[:, 6, 0:NE], iota_p[:, 0:NE], -1.0, float(NE), ALU.mult, ALU.add))
            dve.wait_ge(s_gate, 1)
            link(v.tensor_tensor(gate[0], ps[:, 4, 0:NT * NE].rearrange("p (t e) -> p t e", e=NE),
                                 gb[:, :].unsqueeze(1).to_broadcast([P, NT, NE]), ALU.add))
            link(v.tensor_reduce(prob[0], gate[0], AX.X, ALU.max))
            v.tensor_tensor(gate[1], gate[0], over_e(prob[0]), ALU.subtract).then_inc(s_sub, 1)
            dve.wait_ge(s_exp, 1)
            link(v.tensor_reduce(prob[1], gate[2], AX.X, ALU.add))
            link(v.reciprocal(prob[1], prob[1]))
            link(v.tensor_tensor(gate[0], gate[2], over_e(prob[1]), ALU.mult))
            rank_e = small[:, 6, 0:NE].unsqueeze(1).to_broadcast([P, NT, NE])
            pick = assign.rearrange("p e (c t) -> p c t e", c=2)
            for c in range(2):
                link(v.tensor_reduce(prob[2 + c], gate[0], AX.X, ALU.max))
                link(v.tensor_tensor(gate[1], gate[0], over_e(prob[2 + c]), ALU.is_equal))
                link(v.tensor_tensor(gate[2], gate[1], rank_e, ALU.mult))
                link(v.tensor_reduce(prob[4], gate[2], AX.X, ALU.max))
                link(v.tensor_tensor(gate[3], gate[2], over_e(prob[4]), ALU.is_equal))
                if c == 0:
                    mark(v.scalar_tensor_tensor(gate[0], gate[3], -2.0, gate[0], ALU.mult, ALU.add))
                link(v.tensor_tensor(pick[:, c], gate[3], over_e(valid[:]), ALU.mult))
            flat = assign.rearrange("p e j -> p (e j)")
            link(v.tensor_tensor_scan(a_scan.rearrange("p e j -> p (e j)"), flat, flat, 0.0, ALU.add, ALU.max))
            ends = a_scan[:, :, NA - 1]
            link(v.tensor_copy(small[:, 7, 1:NE], ends[:, 0:NE - 1]))
            link(v.tensor_tensor(cnt16[:, 0:NE], ends, small[:, 7, 0:NE], ALU.subtract))
            dve.sem_inc(s_cnt, 1)
            link(v.tensor_tensor(prob[4], prob[2], prob[3], ALU.add))
            link(v.reciprocal(prob[5], prob[4]))
            mark(v.tensor_tensor(prob[2], prob[2], prob[5], ALU.mult))
            mark(v.tensor_tensor(prob[3], prob[3], prob[5], ALU.mult))
            group_ends(NE, 2, small[:, 5, 0:NE])
            link(v.tensor_tensor(small[:, 5, 0:NE], small[:, 5, 0:NE], small[:, 7, 0:NE], ALU.subtract))
            link(v.tensor_tensor(a_scan, a_scan, small[:, 5, 0:NE].unsqueeze(2).to_broadcast([P, NE, NA]), ALU.add))
            link(v.tensor_tensor(a_scan, a_scan, assign, ALU.mult))
            link(v.tensor_reduce(a_pos, a_scan.rearrange("p e j -> p j e"), AX.X, ALU.add))
            v.tensor_scalar(a_slot, a_pos, -1.0, 0.0, ALU.add, ALU.max).then_inc(s_slot2, 1)
            chunk_map(NE, NST, 2, expert_at[:], 1, NE - 1)

            def rows_lo(i, k):
                dve.wait_ge(s_mth, i * 4 + (k + 1))
                v.tensor_tensor(xs_t[k % 2][:, 1], ps[:, k % 2, 0:D].rearrange("p (k s) -> p k s", k=KD),
                                xs_t[k % 2][:, 0], ALU.subtract).then_inc(s_mtc, 1)

            def gated(i, k):
                dve.wait_ge(s_silu, i * 4 + (k + 1))
                v.scalar_tensor_tensor(h_full[k % 2], h_act[k % 2], factor(k % 4, 1), ps[:, 3 + 2 * (k % 2), :],
                                       ALU.mult, ALU.mult).then_inc(s_hf, 1)

            def hidden_lo(i, k):
                dve.wait_ge(s_hh, i * 4 + (k + 1))
                v.tensor_tensor(h_part[k % 2][:, 1].rearrange("p c s -> p (c s)"), h_full[k % 2],
                                h_part[k % 2][:, 0].rearrange("p c s -> p (c s)"), ALU.subtract).then_inc(s_hm, 1)

            def expert_steps(i, last):
                for k in range(4):
                    if not last or k < 3:
                        gated(i, k + 1)
                    if not last or k < 2:
                        rows_lo(i, k + 2)
                    if not last or k < 3:
                        hidden_lo(i, k + 1)
            rows_lo(0, 0)
            gated(0, 0)
            rows_lo(0, 1)
            hidden_lo(0, 0)
            with dve.Fori(0, NST // 4 - 1) as i:
                expert_steps(i, False)
            expert_steps(NST // 4 - 1, True)
            for t in range(NT):
                dve.wait_ge(s_yg[t % 4], 32 * (t // 4 + 1))
                link(v.scalar_tensor_tensor(x_sb[:, t, :], y_in[:, 2 * (t % 4), :], prob[2][:, t:t + 1], x_sb[:, t, :],
                                            ALU.mult, ALU.add))
                v.scalar_tensor_tensor(x_sb[:, t, :], y_in[:, 2 * (t % 4) + 1, :], prob[3][:, t:t + 1], x_sb[:, t, :],
                                       ALU.mult, ALU.add).then_inc(s_fin, 1)


_INS = ['x', 'src', 'dst', 'edge_type_16', 'L0_gnn_Wf', 'L0_gnn_Wb', 'L0_gnn_loop_weight', 'L0_gnn_forward_bias',
        'L0_gnn_backward_bias', 'L0_gnn_self_bias', 'L0_ffn_gate_w', 'L0_ffn_gate_b', 'L0_ffn_w1', 'L0_ffn_w2',
        'L0_ffn_w3']


def kernel(**inputs):
    import numpy as _np
    import concourse.bacc as _bacc
    from concourse import mybir as _mybir
    from concourse.bass_utils import run_bass_kernel_spmd as _run

    nc = _bacc.Bacc("TRN2", target_bir_lowering=False, num_devices=1)
    arrays, args = {}, []
    for name in _INS:
        a = _np.ascontiguousarray(inputs[name])
        arrays[f"in_{name}"] = a
        args.append(nc.dram_tensor(f"in_{name}", a.shape, _mybir.dt.from_np(a.dtype), kind="ExternalInput").ap())
    args.append(nc.dram_tensor("out_0", (N, D), fp32, kind="ExternalOutput").ap())
    build(nc, *args)
    r = _run(nc, [arrays], core_ids=[0])
    return r.results[0]["out_0"]
```
